# Optimizing a Trainium2 kernel written in Bass

```python
import numpy as np
import jax
import jax.numpy as jnp

def _softmax(x, axis=-1):
    return jax.nn.softmax(x, axis=axis)

def _gelu(x):
    return jax.nn.gelu(x, approximate=True)

def _silu(x):
    return jax.nn.silu(x)

def _sigmoid(x):
    return jax.nn.sigmoid(x)

def _layernorm(x, axis=-1, eps=1e-05):
    m = jnp.mean(x, axis=axis, keepdims=True)
    v = jnp.var(x, axis=axis, keepdims=True)
    return (x - m) / jnp.sqrt(v + eps)

def _scatter_add(tgt, idx, src, axis=0):
    return tgt.at[idx].add(src)

def _segment_sum(src, seg, n):
    return jax.ops.segment_sum(src, seg, n)
kernel_name = 'mk_adj_resnorm_d4_adj_r2_69c4b7'

def setup_inputs(seed: int=0):
    np.random.seed(seed)
    _w = jnp.asarray

    def _rec_inputs():
        import jax
        import jax.numpy as jnp
        _gk = jax.random.key(seed)
        x = -0.0002928 + 1 * jax.random.normal(jax.random.fold_in(_gk, 1), (4096, 256), jnp.float32)
        _w = (1.0 + jnp.arange(4096, dtype=jnp.float32)) ** (-0.5)
        _w = _w / _w.mean()
        _pij = jnp.clip(0.00195312 * _w[:, None] * _w[None, :], 0.0, 1.0)
        _a = jax.random.uniform(jax.random.fold_in(_gk, 2), (4096, 4096)) < _pij
        _a = jnp.logical_or(_a, jnp.swapaxes(_a, -1, -2))
        _a = jnp.logical_or(_a, jnp.eye(4096, dtype=bool))
        _af = _a.astype(jnp.float32)
        _af = _af * jax.random.uniform(jax.random.fold_in(_gk, 3), (4096, 4096), jnp.float32, 0.05, 5.41998)
        adj = _af
        return (x, adj)
    x, adj = _rec_inputs()

    def _L0_gnn_setup():
        import jax, jax.numpy as jnp
        import numpy as np
        N = 4096
        D = 256
        EPS = 1e-12
        key = jax.random.key(seed)
        k1, k2 = jax.random.split(key)
        cur = jax.random.normal(k1, (N, D), dtype=jnp.float32)
        incidence_m = jax.random.normal(k2, (N, N), dtype=jnp.float32)
        return {'cur': cur, 'incidence_m': incidence_m}
    _L0_gnn_all = _L0_gnn_setup()
    _L0_gnn_in = {k: v for k, v in _L0_gnn_all.items() if k in ()}
    del _L0_gnn_all

    def _L1_gnn_setup():
        import jax, jax.numpy as jnp
        import numpy as np
        N = 4096
        D = 256
        key = jax.random.key(seed)
        ks = jax.random.split(key, 6)
        s = 1.0 / np.sqrt(D)
        return {'x': jax.random.normal(ks[0], (N, D), jnp.float32), 'spatial_encoding': jax.random.normal(ks[1], (N, N), jnp.float32), 'edge_encoding': jax.random.normal(ks[2], (N, N), jnp.float32), 'Wq': jax.random.normal(ks[3], (D, D), jnp.float32) * s, 'bq': jnp.zeros((D,), jnp.float32), 'Wk': jax.random.normal(ks[4], (D, D), jnp.float32) * s, 'bk': jnp.zeros((D,), jnp.float32), 'Wv': jax.random.normal(ks[5], (D, D), jnp.float32) * s, 'bv': jnp.zeros((D,), jnp.float32)}
    _L1_gnn_all = _L1_gnn_setup()
    _L1_gnn_in = {k: v for k, v in _L1_gnn_all.items() if k in ('Wq', 'bq', 'Wk', 'bk', 'Wv', 'bv')}
    del _L1_gnn_all

    def _L2_gnn_setup():
        import jax, jax.numpy as jnp
        import numpy as np

        def _bin_sign(v):
            return jnp.sign(v)

        def _bin_sign_z(v):
            return jnp.maximum(jnp.sign(v), 0.0)
        key = jax.random.key(seed)
        k1, k2, k3 = jax.random.split(key, 3)
        N, D_IN, D_OUT = (4096, 256, 256)
        x = jax.random.normal(k1, (N, D_IN), dtype=jnp.float32)
        support = jax.random.uniform(k2, (N, N), dtype=jnp.float32)
        weight = jax.random.normal(k3, (D_OUT, D_IN), dtype=jnp.float32)
        return {'x': x, 'support': support, 'weight': weight}
    _L2_gnn_all = _L2_gnn_setup()
    _L2_gnn_in = {k: v for k, v in _L2_gnn_all.items() if k in ('weight',)}
    del _L2_gnn_all

    def _L3_gnn_setup():
        import jax, jax.numpy as jnp
        import numpy as np
        N = 4096
        IN_F = 256
        OUT_F = 256
        key = jax.random.key(seed)
        k_x, k_adj, k_w = jax.random.split(key, 3)
        x = jax.random.normal(k_x, (N, IN_F), dtype=jnp.float32)
        adj = jax.random.uniform(k_adj, (N, N), dtype=jnp.float32)
        stdv = 1.0 / np.sqrt(OUT_F)
        weight = jax.random.uniform(k_w, (IN_F, OUT_F), dtype=jnp.float32, minval=-stdv, maxval=stdv)
        return {'x': x, 'adj': adj, 'weight': weight}
    _L3_gnn_all = _L3_gnn_setup()
    _L3_gnn_in = {k: v for k, v in _L3_gnn_all.items() if k in ('weight',)}
    del _L3_gnn_all
    return {'x': x, 'adj': adj, 'L1_gnn_Wq': _L1_gnn_in['Wq'], 'L1_gnn_bq': _L1_gnn_in['bq'], 'L1_gnn_Wk': _L1_gnn_in['Wk'], 'L1_gnn_bk': _L1_gnn_in['bk'], 'L1_gnn_Wv': _L1_gnn_in['Wv'], 'L1_gnn_bv': _L1_gnn_in['bv'], 'L2_gnn_weight': _L2_gnn_in['weight'], 'L3_gnn_weight': _L3_gnn_in['weight']}

def reference(x, adj, L1_gnn_Wq, L1_gnn_bq, L1_gnn_Wk, L1_gnn_bk, L1_gnn_Wv, L1_gnn_bv, L2_gnn_weight, L3_gnn_weight):
    import jax
    import jax.numpy as jnp

    def _L0_gnn_ref(cur, incidence_m):
        import jax, jax.numpy as jnp
        import numpy as np
        N = 4096
        D = 256
        EPS = 1e-12
        mask = incidence_m > 0
        head = jax.lax.stop_gradient(mask.astype(incidence_m.dtype))
        head = head / jnp.maximum(jnp.sqrt(jnp.sum(head * head, axis=-1, keepdims=True)), EPS)
        inc = incidence_m + head
        edge_fea = inc @ cur
        edge_degree = jnp.sum(inc, axis=-1, keepdims=True)
        return edge_fea / edge_degree

    def _L1_gnn_ref(x, spatial_encoding, edge_encoding, Wq, bq, Wk, bk, Wv, bv):
        import jax, jax.numpy as jnp
        import numpy as np
        N = 4096
        D = 256
        q = x @ Wq.T + bq
        k = x @ Wk.T + bk
        v = x @ Wv.T + bv
        scale = 1.0 / jnp.sqrt(jnp.asarray(q.shape[-1], q.dtype))
        a = q @ k.T * scale + spatial_encoding + edge_encoding
        attn = jax.nn.softmax(a, axis=-1)
        return attn @ v

    def _L2_gnn_ref(x, support, weight):
        import jax, jax.numpy as jnp
        import numpy as np

        def _bin_sign(v):
            return jnp.sign(v)

        def _bin_sign_z(v):
            return jnp.maximum(jnp.sign(v), 0.0)
        bw = _bin_sign(weight)
        ba = _bin_sign_z(x)
        xw = ba @ bw.T
        out = support @ xw
        return jax.nn.relu(out)

    def _L3_gnn_ref(x, adj, weight):
        import jax, jax.numpy as jnp
        import numpy as np
        N = 4096
        IN_F = 256
        OUT_F = 256
        n = adj.shape[0]
        adj_hat = adj + jnp.eye(n, dtype=adj.dtype)
        rowsum = adj_hat.sum(axis=1)
        d_inv_sqrt = jnp.power(rowsum, -0.5)
        d_inv_sqrt = jnp.where(jnp.isinf(d_inv_sqrt), 0.0, d_inv_sqrt)
        adj_norm = adj_hat * d_inv_sqrt[:, None] * d_inv_sqrt[None, :]
        support = x @ weight
        out = adj_norm @ support
        return jax.nn.relu(out)
    x = _layernorm(x + _L0_gnn_ref(x, adj), axis=-1)
    x = _layernorm(x + _L1_gnn_ref(x, adj, adj, L1_gnn_Wq, L1_gnn_bq, L1_gnn_Wk, L1_gnn_bk, L1_gnn_Wv, L1_gnn_bv), axis=-1)
    x = _layernorm(x + _L2_gnn_ref(x, adj, L2_gnn_weight), axis=-1)
    x = _layernorm(x + _L3_gnn_ref(x, adj, L3_gnn_weight), axis=-1)
    return x

_drawn_inputs = setup_inputs


def setup_inputs(seed=0):
    import zlib

    import numpy as np

    out = dict(_drawn_inputs(seed))
    spreads = {'L1_gnn_bq': (0.0, 0.1), 'L1_gnn_bk': (0.0, 0.1), 'L1_gnn_bv': (0.0, 0.1)}
    factors = {}
    for name, (base, spread) in spreads.items():
        noise = np.random.default_rng([zlib.crc32(name.encode()), seed]).standard_normal(out[name].shape)
        drawn = base * np.exp(spread * noise) if base else spread * noise
        out[name] = jnp.asarray(drawn.astype(out[name].dtype))
    for name, factor in factors.items():
        out[name] = (out[name] * factor).astype(out[name].dtype)
    return out
```

```python
import concourse.bass as bass
from concourse import mybir
from contextlib import ExitStack

P = 128
N = 4096
D = 256
NB = N // P
CHUNKS = 8
CW = N // CHUNKS
TPC = CW // P
PIECES = 4
PW = N // PIECES
TPP = PW // P
DC = D // P
LN_EPS = 1e-5
HEAD_EPS = 1e-12
PAIRS = NB // 2
CONSTANTS = (0.5, -0.5, LN_EPS, 1.0, 0.0)
C_HALF, C_MHALF, C_LN_EPS, C_ONE, C_ZERO = range(len(CONSTANTS))

F32 = mybir.dt.float32
F32R = mybir.dt.float32r
BF16 = mybir.dt.bfloat16
U8 = mybir.dt.uint8
ALU = mybir.AluOpType
ACT = mybir.ActivationFunctionType
AX = mybir.AxisListType


class Blk:

    def __init__(self, n, off):
        self.n, self.off = n, off
        self.par = off % 2

    def at(self, shift):
        return Blk(self.n, self.off + shift)

    @property
    def number(self):
        return 2 * self.n + self.off

    def exists(self):
        return not isinstance(self.n, int) or 0 <= self.number < NB

    def after(self, per_block, k):
        return 2 * per_block * self.n + per_block * self.off + k

    def needs(self, per_block, k):
        return not isinstance(self.n, int) or self.after(per_block, k) > 0

    def landed(self, layer=0):
        return 16 * self.n + 16 * (self.off // 2 + 1 + PAIRS * layer)

    def rows(self):
        return self.number


def build(nc, x_in, adj, adjT, wkqv, bias, w2t, w3, ident_in, out):
    ctx = ExitStack()
    with ctx:
        def sb(name, shape, dt):
            return ctx.enter_context(nc.sbuf_tensor(name, shape, dt))

        def overlay(*groups):
            made = []
            for i, group in enumerate(groups):
                stack = ctx if i == len(groups) - 1 else ExitStack()
                made += [stack.enter_context(nc.sbuf_tensor(*t)) for t in group]
                if stack is not ctx:
                    stack.close()
            return made

        def sem(name):
            return ctx.enter_context(nc.semaphore(name))

        ident = sb("ident", [P, P], F32)
        ones = sb("ones", [P, P], F32R)
        const = sb("const", [P, len(CONSTANTS)], F32)
        dinv = sb("dinv", [P, NB], F32)
        xhl, vhl, yhl = overlay([("xhl", [P, NB, 2 * D], F32R)], [("vhl", [P, NB, 2 * D], F32R)],
                                [("yhl", [P, NB, 2 * D], F32R)])
        x_stage, w_stage, b_stage, xw, piece_hl, kT = overlay(
            [("x_stage", [P, NB, D], F32), ("w_stage", [P, DC, 3 * D], F32), ("b_stage", [P, 3 * D], F32)],
            [("xw", [P, NB, D], F32R), ("piece_hl", [P, PIECES, 2, PW], F32R)],
            [("kT", [P, 2, DC, N], F32R)])
        a_buf = [sb(f"a_buf{i}", [P, N], F32) for i in range(2)]
        chunk_hl = sb("chunk_hl", [P, 4, 2, CW], F32R)
        xres = sb("xres", [P, 2, D], F32)
        u = sb("u", [P, D], F32)
        xn = sb("xn", [P, 2, D], F32)
        xT = sb("xT", [P, 2, DC, P], F32R)
        settle = sb("settle", [1, CHUNKS + 1], F32)
        bn6 = sb("bn6", [P, 6], F32)
        mv = sb("mv", [P, 2], F32)
        norm = sb("norm", [P, 4], F32)
        part = sb("part", [P, 2, 2, PIECES], F32)
        st = sb("st", [P, 2, 16], F32)
        rr = sb("rr", [P, 2, 4], F32)
        qt = sb("qt", [P, 2, 2, D], F32R)
        mxp = sb("mxp", [P, 2, CHUNKS], F32)
        mx = sb("mx", [P, 2, 2], F32)
        lp = sb("lp", [P, 2, PIECES], F32)
        ls = sb("ls", [P, 2], F32)
        (w2_stage, w3_stage, w3_hl, w2_sign, ba, baT, xw_out,
         w_hl, b_r, w_mask, junk_dve, junk_act, kq_hl, v_hl) = overlay(
            [("w2_stage", [P, DC, D], F32), ("w3_stage", [P, DC, D], F32), ("w3_hl", [P, 2, DC, D], F32R),
             ("w2_sign", [P, DC, D], F32R), ("ba", [P, D], F32), ("baT", [P, DC, P], F32R),
             ("xw_out", [P, D], F32R)],
            [("w_hl", [P, 2, DC, 3 * D], F32R), ("b_r", [P, 3 * D], F32R), ("w_mask", [P, 2, CW], F32),
             ("junk_dve", [P, PW], U8), ("junk_act", [P, PW], BF16), ("kq_hl", [P, 2, 2 * D], F32R),
             ("v_hl", [P, 2 * D], F32R)])

        banks = [ctx.enter_context(nc.psum_tensor(f"bank{i}", [P, 512], F32)) for i in range(8)]
        T0 = banks[0:4]
        S1, T1 = banks[0:2], banks[2:4]
        O = banks[4:6]
        E0, E1 = banks[6], banks[7]

        def dram(name, shape, dt):
            return nc.dram_tensor(name, shape, dt).ap()

        def f32(ap):
            return ap.bitcast(F32)

        x_mid = [dram(f"x_mid{i}", [N, D], F32) for i in range(3)]
        x_of = [x_in] + x_mid + [out]
        q_scr = dram("q_scr", [NB, P, 2, D], F32)
        v_scr = dram("v_scr", [NB, P, 2 * D], F32)
        xw_scr = dram("xw_scr", [NB, P, D], F32)

        def x_rows(layer, b):
            return x_of[layer].rearrange("(b p) d -> b p d", p=P)[b.rows()]

        const_in = sem("const_in")
        bias_in = sem("bias_in")
        x_stage_in = [sem(f"x_stage_in{c}") for c in range(CHUNKS)]
        a_in = [[sem(f"a_in{par}_{p}") for p in range(PIECES)] for par in range(2)]
        xres_in = [sem(f"xres_in{par}") for par in range(2)]
        x_out = [sem(f"x_out{par}") for par in range(2)]
        k_placed, q_stored, v_stored = sem("k_placed"), sem("q_stored"), sem("v_stored")
        q_in = [sem(f"q_in{par}") for par in range(2)]
        v_in = [sem(f"v_in{c}") for c in range(CHUNKS)]
        w23_in = sem("w23_in")
        xw_stored = sem("xw_stored")
        xw_in = sem("xw_in")
        memsets = sem("memsets")
        x_hi, x_lo = sem("x_hi"), sem("x_lo")
        w_hi, w_lo = sem("w_hi"), sem("w_lo")
        bias_ready = sem("bias_ready")
        w23_ready, w3_hi = sem("w23_ready"), sem("w3_hi")
        counted = sem("counted")
        summed = sem("summed")
        stats = sem("stats")
        head_scale = sem("head_scale")
        rdeg = sem("rdeg")
        masked = sem("masked")
        t0_done = sem("t0_done")
        hi0, lo0 = sem("hi0"), sem("lo0")
        mm0 = sem("mm0")
        kqv_mm = sem("kqv_mm")
        kq_hi, kq_lo, v_hi, v_lo = sem("kq_hi"), sem("kq_lo"), sem("v_hi"), sem("v_lo")
        qk_done = sem("qk_done")
        scored = sem("scored")
        maxed = sem("maxed")
        exped = sem("exped")
        t1_done = sem("t1_done")
        hi1, lo1 = sem("hi1"), sem("lo1")
        pv_done = sem("pv_done")
        bin_done, binT_done = sem("bin_done"), sem("binT_done")
        xw_mm, xw_copied = sem("xw_mm"), sem("xw_copied")
        hi2, lo2, mm2 = sem("hi2"), sem("lo2"), sem("mm2")
        y_mm, y_hi, y_lo = sem("y_mm"), sem("y_hi"), sem("y_lo")
        LN_STEPS = [4, 6, 3, 7]
        ln = [sem(f"ln{i}") for i in range(4)]
        normed = sem("normed")
        xn_done = sem("xn_done")
        xT_done = sem("xT_done")
        xT_hi, xT_lo = sem("xT_hi"), sem("xT_lo")

        block = ctx.enter_context(nc.Block())

        def ahead(layer, b, k):
            if not isinstance(b.n, int):
                return layer, b.at(k)
            return layer + (b.number + k) // NB, Blk(0, (b.number + k) % NB)

        def over(b, layer, per_block, k):
            return b.after(per_block, k) + per_block * NB * layer

        @block.sync
        def _(sp):
            def load_a(layer, b, p):
                sp.dma_start(a_buf[b.par][:, p * PW:(p + 1) * PW],
                             (adj.rearrange("(b p) n -> b p n", p=P) if layer < 2 else adjT)[b.rows()]
                             [:, p * PW:(p + 1) * PW]).then_inc(a_in[b.par][p], 16)

            def load_xres(layer, b):
                if layer > 0:
                    sp.wait_ge(x_out[b.par], 16 * PAIRS * layer)
                sp.dma_start(xres[:, b.par, :], x_rows(layer, b)).then_inc(xres_in[b.par], 16)

            def store_x(layer, b):
                sp.wait_ge(xn_done, over(b, layer, 1, 1))
                sp.dma_start(x_rows(layer + 1, b), xn[:, b.par, :]).then_inc(x_out[b.par], 16)

            def read0(b, p):
                sp.wait_ge(hi0, b.after(8, 2 * p + 2))

            def store_kqv(b):
                i = b.rows()
                sp.wait_ge(kq_hi, b.after(1, 1))
                sp.wait_ge(kq_lo, b.after(1, 1))
                for h in range(2):
                    sp.dma_start(f32(kT[:, h, :, bass.ds(i * P, P)]),
                                 f32(kq_hl[:, h, 0:D]).rearrange("p (c n) -> p c n", c=DC)).then_inc(k_placed, 16)
                sp.dma_start(q_scr[i], f32(kq_hl[:, :, D:2 * D])).then_inc(q_stored, 16)
                sp.wait_ge(v_lo, b.after(1, 1))
                sp.dma_start(v_scr[i], f32(v_hl[:, :])).then_inc(v_stored, 16)

            def body0(b, layer, nxt):
                if b.needs(1, -1):
                    sp.wait_ge(ln[0], b.at(-2).after(4, 2))
                load_xres(0, b)
                for p in range(2):
                    read0(b, p)
                    load_a(layer, nxt, p)
                if b.at(-1).exists():
                    store_x(0, b.at(-1))
                read0(b, 2)
                load_a(layer, nxt, 2)
                if b.at(-1).exists():
                    store_kqv(b.at(-1))
                read0(b, 3)
                load_a(layer, nxt, 3)

            first, second = Blk(0, 0), Blk(0, 1)
            sp.dma_start(a_buf[0][:, 0:PW], adj[0:P, 0:PW]).then_inc(a_in[0][0], 16)
            for c in range(1):
                sp.dma_start(x_stage[:, c * TPC:(c + 1) * TPC, :],
                             x_in.rearrange("(t p) d -> p t d", p=P)[:, c * TPC:(c + 1) * TPC, :]
                             ).then_inc(x_stage_in[c], 16)
            sp.dma_start(ident[:, :], ident_in).then_inc(const_in, 16)
            for p in range(1, PIECES):
                load_a(0, first, p)
            for c in range(1, CHUNKS):
                sp.dma_start(x_stage[:, c * TPC:(c + 1) * TPC, :],
                             x_in.rearrange("(t p) d -> p t d", p=P)[:, c * TPC:(c + 1) * TPC, :]
                             ).then_inc(x_stage_in[c], 16)
            sp.dma_start(w_stage[:, :, :], wkqv.rearrange("(c p) n -> p c n", p=P)).then_inc(const_in, 16)
            sp.wait_ge(memsets, 3)
            sp.dma_start(b_stage[0:1, :], bias).then_inc(bias_in, 16)
            sp.dma_start(b_stage[32:33, :], bias).then_inc(bias_in, 16)
            for p in range(PIECES):
                load_a(0, second, p)

            for off in range(2):
                body0(Blk(0, off), 0, Blk(0, off + 2))
            with sp.Fori(1, PAIRS - 1) as n:
                for off in range(2):
                    body0(Blk(n, off), 0, Blk(n, off + 2))
            for off in range(2):
                body0(Blk(PAIRS - 1, off), 1, Blk(0, off))

            def load_q(b):
                sp.wait_ge(q_stored, 16 * NB if not isinstance(b.n, int) or b.number > 1
                           else 16 * (NB - 1) if b.number == 0 else 16 * NB)
                sp.dma_start(f32(qt[:, b.par, :, :]), q_scr[b.rows()]).then_inc(q_in[b.par], 16)

            def store_xw(b):
                sp.wait_ge(xw_copied, b.after(1, 1))
                sp.dma_start(xw_scr[b.rows()], f32(xw_out[:, :])).then_inc(xw_stored, 16)

            def body1(b, nxt, layer):
                if b.at(-2).exists():
                    sp.wait_ge(t1_done, b.at(-2).after(8, 8))
                    load_a(1, b, 3)
                if b.needs(1, 0):
                    sp.wait_ge(qk_done, b.at(-1).after(8, 8))
                if b.at(1).exists() or not isinstance(b.n, int):
                    load_q(nxt)
                for p in range(3):
                    if b.at(-1).exists():
                        sp.wait_ge(t1_done, b.at(-1).after(8, 2 * p + 2))
                        load_a(layer, nxt, p)
                    if p == 0:
                        if b.at(-2).exists():
                            store_x(1, b.at(-2))
                            sp.wait_ge(ln[1], b.at(-2).after(6, 4))
                        else:
                            sp.wait_ge(ln[0], 4 * (NB - 2 + b.number) + 2)
                        load_xres(1, b)
                if b.at(-2).exists():
                    store_xw(b.at(-2))

            load_q(Blk(0, 0))
            sp.wait_ge(mm0, 8 * NB)
            sp.wait_ge(v_stored, 16 * (NB - 1))
            for c in range(CHUNKS - 1):
                sp.dma_start(f32(vhl[:, c * TPC:(c + 1) * TPC, :]),
                             v_scr.rearrange("b p n -> p b n")[:, c * TPC:(c + 1) * TPC, :]).then_inc(v_in[c], 16)
            store_x(0, Blk(0, NB - 1))
            store_kqv(Blk(0, NB - 1))
            sp.wait_ge(v_stored, 16 * NB)
            c = CHUNKS - 1
            sp.dma_start(f32(vhl[:, c * TPC:(c + 1) * TPC, :]),
                         v_scr.rearrange("b p n -> p b n")[:, c * TPC:(c + 1) * TPC, :]).then_inc(v_in[c], 16)
            sp.wait_ge(k_placed, 32 * NB)
            sp.wait_ge(q_stored, 16 * NB)
            sp.wait_ge(kqv_mm, 2 * NB)
            sp.dma_start(w2_stage[:, :, :], w2t.rearrange("(c p) n -> p c n", p=P)).then_inc(w23_in, 16)
            sp.dma_start(w3_stage[:, :, :], w3.rearrange("(c p) n -> p c n", p=P)).then_inc(w23_in, 16)
            for off in range(2):
                body1(Blk(0, off), Blk(0, off + 1), 1)
            with sp.Fori(1, PAIRS - 1) as n:
                for off in range(2):
                    body1(Blk(n, off), Blk(n, off + 1), 1)
            body1(Blk(PAIRS - 1, 0), Blk(PAIRS - 1, 1), 1)
            last = Blk(0, NB - 1)
            sp.wait_ge(t1_done, last.at(-2).after(8, 8))
            load_a(1, last, 3)
            for p in range(PIECES):
                sp.wait_ge(t1_done, last.at(-1).after(8, 2 * p + 2))
                load_a(2, Blk(0, 0), p)
                if p == 0:
                    store_x(1, last.at(-2))
                    sp.wait_ge(ln[1], last.at(-2).after(6, 4))
                    load_xres(1, last)
                if p == 2:
                    store_xw(last.at(-2))
            sp.wait_ge(qk_done, 8 * NB)
            sp.wait_ge(xw_stored, 16 * (NB - 2))
            sp.dma_start(f32(xw[:, 0:NB - 2, :]), xw_scr.rearrange("b p n -> p b n")[:, 0:NB - 2, :]).then_inc(xw_in, 16)
            store_x(1, last.at(-1))
            sp.wait_ge(ln[1], last.at(-1).after(6, 4))
            load_xres(2, Blk(0, 0))
            sp.wait_ge(xw_copied, NB - 1)
            sp.dma_start(f32(xw[:, NB - 2, :]), f32(xw_out[:, :])).then_inc(xw_stored, 16)
            for p in range(PIECES):
                sp.wait_ge(t1_done, last.after(8, 2 * p + 2))
                load_a(2, Blk(0, 1), p)
            for p in range(PIECES):
                sp.wait_ge(lo2, p + 1)
                load_a(2, Blk(0, 2), p)

            def body2(layer, b):
                for p in range(PIECES):
                    to_layer, to = ahead(layer, b, 3)
                    if to_layer < 4:
                        sp.wait_ge(lo2, over(b.at(1), layer - 2, 4, p + 1))
                        load_a(to_layer, to, p)
                    if p == 0:
                        prev_layer, prev = ahead(layer, b, -1)
                        store_x(prev_layer, prev)
                        if (prev_layer, layer) == (1, 2):
                            sp.wait_ge(xw_copied, NB)
                            sp.dma_start(f32(xw[:, NB - 1, :]), f32(xw_out[:, :])).then_inc(xw_stored, 16)
                        to_layer, to = ahead(layer, b, 1)
                        if to_layer < 4:
                            steps = LN_STEPS[prev_layer]
                            sp.wait_ge(ln[prev_layer], prev.after(steps, steps - 2))
                            load_xres(to_layer, to)

            for layer in (2, 3):
                for off in range(2):
                    body2(layer, Blk(0, off))
                with sp.Fori(1, PAIRS - 2) as n:
                    for off in range(2):
                        body2(layer, Blk(n, off))
                for off in range(4):
                    body2(layer, Blk(PAIRS - 2, off))
            store_x(3, last)
            for par in range(2):
                sp.wait_ge(x_out[par], 16 * PAIRS * 4)
            sp.wait_ge(xw_stored, 16 * NB)

        @block.tensor
        def _(pe):
            def transpose0(b, c):
                pe.wait_ge(masked, b.after(8, c + 1))
                if b.needs(8, c - 3):
                    pe.wait_ge(lo0, b.after(8, c - 3))
                for t in range(TPC):
                    cols = slice(t * P, (t + 1) * P)
                    pe.matmul(T0[c % 4][:, cols], a_buf[b.par][:, c * CW + t * P:c * CW + (t + 1) * P],
                              ident[:, :], start=True, stop=False, is_transpose=True)
                    mm = pe.matmul(T0[c % 4][:, cols], w_mask[:, c % 2, cols], ident[:, :],
                                   start=False, stop=True, is_transpose=True)
                mm.then_inc(t0_done, 1)

            def by_hi_lo(b, c, values, done):
                o = O[b.par]
                for t in range(TPC):
                    j = c * TPC + t
                    hi = chunk_hl[:, c % 4, 0, t * P:(t + 1) * P]
                    lo = chunk_hl[:, c % 4, 1, t * P:(t + 1) * P]
                    if j < NB - 1:
                        pe.matmul(o[:, :], hi, values[:, j, :], start=(j == 0), stop=False)
                        mm = pe.matmul(o[:, D:2 * D], lo, values[:, j, 0:D], start=False, stop=False)
                    else:
                        pe.matmul(o[:, D:2 * D], lo, values[:, j, 0:D], start=False, stop=False)
                        mm = pe.matmul(o[:, :], hi, values[:, j, :], start=False, stop=True)
                mm.then_inc(done, 1)

            def products0(b, c):
                pe.wait_ge(lo0, b.after(8, c + 1))
                if isinstance(b.n, int) and b.number == 0:
                    pe.wait_ge(x_lo, c + 1)
                if c == 0 and b.needs(1, -1):
                    pe.wait_ge(ln[0], b.at(-2).after(4, 2))
                by_hi_lo(b, c, xhl, mm0)

            def block_transpose(layer, b, src, ready, value):
                pe.wait_ge(ready, value)
                for dc in range(DC):
                    mm = pe.transpose(E0[:, dc * P:(dc + 1) * P], src[:, dc * P:(dc + 1) * P], ident[:, :])
                mm.then_inc(xT_done, 1)

            def end0_transpose(b):
                if b.needs(1, 0):
                    pe.wait_ge(v_lo, b.after(1, 0))
                block_transpose(0, b, xn[:, b.par, :], xn_done, b.after(1, 1))

            def end0_kqv(b):
                pe.wait_ge(xT_hi, b.after(1, 1))
                pe.wait_ge(xT_lo, b.after(1, 1))
                if isinstance(b.n, int) and b.number == 0:
                    pe.wait_ge(w_lo, 3)
                    pe.wait_ge(bias_ready, 3)
                if b.needs(1, 0):
                    pe.wait_ge(kq_lo, b.after(1, 0))
                for g in range(4):
                    cols = slice(g * P, (g + 1) * P)
                    pe.matmul(E1[:, cols], b_r[:, cols], ones[:, :], start=True, stop=False)
                    for dc in range(DC):
                        pe.matmul(E1[:, cols], w_hl[:, 1, dc, cols], xT[:, 0, dc, :], start=False, stop=False)
                        pe.matmul(E1[:, cols], w_hl[:, 0, dc, cols], xT[:, 1, dc, :], start=False, stop=False)
                        mm = pe.matmul(E1[:, cols], w_hl[:, 0, dc, cols], xT[:, 0, dc, :],
                                       start=False, stop=(dc == DC - 1))
                mm.then_inc(kqv_mm, 1)
                v = slice(2 * D, 3 * D)
                pe.matmul(E0[:, 0:D], ones[:, :], b_r[:, v], start=True, stop=False)
                for dc in range(DC):
                    pe.matmul(E0[:, 0:D], xT[:, 1, dc, :], w_hl[:, 0, dc, v], start=False, stop=False)
                    pe.matmul(E0[:, 0:D], xT[:, 0, dc, :], w_hl[:, 1, dc, v], start=False, stop=False)
                    mm = pe.matmul(E0[:, 0:D], xT[:, 0, dc, :], w_hl[:, 0, dc, v],
                                   start=False, stop=(dc == DC - 1))
                mm.then_inc(kqv_mm, 1)

            def slot0(b, c):
                if b.exists():
                    transpose0(b, c)
                prev = b if c >= 2 else b.at(-1)
                if prev.exists():
                    products0(prev, (c - 2) % CHUNKS)
                if b.at(-1).exists():
                    if c == 4:
                        end0_transpose(b.at(-1))
                    if c == 6:
                        end0_kqv(b.at(-1))

            pe.wait_ge(const_in, 16)
            pe.wait_ge(memsets, 1)
            for off in range(2):
                for c in range(CHUNKS):
                    slot0(Blk(0, off), c)
            with pe.Fori(1, PAIRS) as n:
                for off in range(2):
                    for c in range(CHUNKS):
                        slot0(Blk(n, off), c)

            def scores(b, c):
                s = S1[c % 2]
                if c == 0:
                    pe.wait_ge(q_in[b.par], b.landed())
                if isinstance(b.n, int) and b.number == 0:
                    pe.wait_ge(k_placed, 32 * NB if c == CHUNKS - 1 else 32 * (NB - 1))
                    if c == 0:
                        pe.wait_ge(lo0, 8 * NB)
                if b.needs(8, c - 1):
                    pe.wait_ge(scored, b.after(8, c - 1))
                q = qt[:, b.par, :, :]
                cols = slice(c * CW, (c + 1) * CW)
                for dc in range(DC):
                    dd = slice(dc * P, (dc + 1) * P)
                    pe.matmul(s[:, :], q[:, 1, dd], kT[:, 0, dc, cols], start=(dc == 0), stop=False)
                    pe.matmul(s[:, :], q[:, 0, dd], kT[:, 1, dc, cols], start=False, stop=False)
                    mm = pe.matmul(s[:, :], q[:, 0, dd], kT[:, 0, dc, cols], start=False, stop=(dc == DC - 1))
                mm.then_inc(qk_done, 1)

            def transpose1(b, c):
                pe.wait_ge(exped, b.after(4, c // 2 + 1))
                if b.needs(8, c - 1):
                    pe.wait_ge(lo1, b.after(8, c - 1))
                for t in range(TPC):
                    mm = pe.transpose(T1[c % 2][:, t * P:(t + 1) * P],
                                      a_buf[b.par][:, c * CW + t * P:c * CW + (t + 1) * P], ident[:, :])
                mm.then_inc(t1_done, 1)

            def products1(b, c):
                pe.wait_ge(lo1, b.after(8, c + 1))
                if isinstance(b.n, int) and b.number == 0:
                    pe.wait_ge(v_in[c], 16)
                    if c == 0:
                        pe.wait_ge(ln[0], 4 * NB)
                by_hi_lo(b, c, vhl, pv_done)

            def end1_transpose(b):
                if b.needs(1, 0):
                    pe.wait_ge(xw_copied, b.after(1, 0))
                block_transpose(1, b, ba, bin_done, b.after(1, 1))

            def end1_xw(b):
                pe.wait_ge(binT_done, b.after(1, 1))
                if isinstance(b.n, int) and b.number == 0:
                    pe.wait_ge(w23_ready, 2)
                for dc in range(DC):
                    mm = pe.matmul(E0[:, 0:D], baT[:, dc, :], w2_sign[:, dc, :], start=(dc == 0), stop=(dc == 1))
                mm.then_inc(xw_mm, 1)

            def slot1(b, c):
                if b.exists():
                    scores(b, c)
                t = b.at(-1) if c >= 1 else b.at(-2)
                if t.exists():
                    transpose1(t, (c - 1) % CHUNKS)
                m = b.at(-1) if c >= 2 else b.at(-2)
                if m.exists():
                    products1(m, (c - 2) % CHUNKS)
                if b.at(-2).exists():
                    if c == 5:
                        end1_transpose(b.at(-2))
                    if c == 6:
                        end1_xw(b.at(-2))

            for off in range(2):
                for c in range(CHUNKS):
                    if off == 0:
                        if c < 2:
                            products0(Blk(0, NB - 1), c + 6)
                        if c == 4:
                            end0_transpose(Blk(0, NB - 1))
                        if c == 6:
                            end0_kqv(Blk(0, NB - 1))
                    slot1(Blk(0, off), c)
            with pe.Fori(1, PAIRS) as n:
                for off in range(2):
                    for c in range(CHUNKS):
                        slot1(Blk(n, off), c)
            for c in range(CHUNKS):
                slot1(Blk(0, NB), c)
            for c in range(2):
                slot1(Blk(0, NB + 1), c)

            def products2(layer, b, p):
                pe.wait_ge(lo2, over(b, layer - 2, 4, p + 1))
                if layer == 2 and isinstance(b.n, int) and b.number == 0:
                    if p == 0:
                        pe.wait_ge(xw_in, 16)
                    if p == PIECES - 1:
                        pe.wait_ge(xw_stored, 16 * NB)
                if layer == 3 and isinstance(b.n, int) and b.number == 0:
                    pe.wait_ge(y_lo, NB if p == PIECES - 1 else NB - 1)
                if p == 0:
                    before = b.at(-2)
                    if b.needs(1, -1):
                        pe.wait_ge(ln[layer], before.after(LN_STEPS[layer], LN_STEPS[layer] - 2))
                    else:
                        pe.wait_ge(ln[layer - 1], LN_STEPS[layer - 1] * (NB + b.number - 1) - 2)
                o = O[b.par]
                for t in range(TPP):
                    j = p * TPP + t
                    hi = piece_hl[:, p, 0, t * P:(t + 1) * P]
                    lo = piece_hl[:, p, 1, t * P:(t + 1) * P]
                    if layer == 2:
                        pe.matmul(o[:, 0:D], hi, xw[:, j, :], start=(j == 0), stop=False)
                        mm = pe.matmul(o[:, 0:D], lo, xw[:, j, :], start=False, stop=(j == NB - 1))
                    elif j < NB - 1:
                        pe.matmul(o[:, :], hi, yhl[:, j, :], start=(j == 0), stop=False)
                        mm = pe.matmul(o[:, D:2 * D], lo, yhl[:, j, 0:D], start=False, stop=False)
                    else:
                        pe.matmul(o[:, D:2 * D], lo, yhl[:, j, 0:D], start=False, stop=False)
                        mm = pe.matmul(o[:, :], hi, yhl[:, j, :], start=False, stop=True)
                mm.then_inc(mm2, 1)

            def end2_transpose(b):
                if b.needs(1, 0):
                    pe.wait_ge(y_lo, b.after(1, 0))
                else:
                    pe.wait_ge(xw_copied, NB)
                block_transpose(2, b, xn[:, b.par, :], xn_done, over(b, 2, 1, 1))

            def end2_y(b):
                pe.wait_ge(xT_hi, over(b, 1, 1, 1))
                pe.wait_ge(xT_lo, over(b, 1, 1, 1))
                for dc in range(DC):
                    pe.matmul(E0[:, 0:D], xT[:, 1, dc, :], w3_hl[:, 0, dc, :], start=(dc == 0), stop=False)
                    pe.matmul(E0[:, 0:D], xT[:, 0, dc, :], w3_hl[:, 1, dc, :], start=False, stop=False)
                    mm = pe.matmul(E0[:, 0:D], xT[:, 0, dc, :], w3_hl[:, 0, dc, :],
                                   start=False, stop=(dc == DC - 1))
                mm.then_inc(y_mm, 1)

            def body2(layer, b):
                prev_layer, prev = ahead(layer, b, -1)
                for p in range(PIECES):
                    products2(layer, b, p)
                    if prev_layer == 1:
                        if p < 2:
                            (end1_transpose, end1_xw)[p](prev)
                    elif prev_layer == 2:
                        if p == 0:
                            end2_transpose(prev)
                        if p == 2:
                            end2_y(prev)

            for layer in (2, 3):
                for off in range(2):
                    body2(layer, Blk(0, off))
                with pe.Fori(1, PAIRS) as n:
                    for off in range(2):
                        body2(layer, Blk(n, off))

        @block.scalar
        def _(act):
            def row_sum(b, p):
                act.wait_ge(a_in[b.par][p], b.landed())
                if b.needs(1, -1):
                    act.wait_ge(stats, b.at(-2).after(10, 1))
                if b.needs(4, p):
                    act.wait_ge(summed, b.after(4, p))
                act.activation(junk_act[:, :], a_buf[b.par][:, p * PW:(p + 1) * PW], ACT.Copy,
                               accum_out=part[:, b.par, 1, p:p + 1]).then_inc(summed, 1)

            def chunk_hi(b, c, transposed, used, t_bank, out_sem):
                act.wait_ge(transposed, b.after(8, c + 1))
                if b.needs(8, c - 3):
                    act.wait_ge(used, b.after(8, c - 3))
                act.activation(chunk_hl[:, c % 4, 0, :], t_bank[:, :], ACT.Copy).then_inc(out_sem, 1)

            def normalise(layer, b):
                act.wait_ge(normed, over(b, layer, 4, 4))
                if layer > 0 or b.needs(1, -1):
                    act.wait_ge(x_out[b.par], b.at(-2).landed(layer))
                if layer == 0 and b.needs(1, -1):
                    act.wait_ge(xT_done, b.at(-2).after(1, 1))
                act.activation(xn[:, b.par, :], u[:, :], ACT.Identity, bias=norm[:, 2:3],
                               scale=norm[:, 1:2]).then_inc(xn_done, 1)

            def split_xT(b, t_value, s_value, used, used_value):
                act.wait_ge(xT_done, t_value)
                if used is not None:
                    act.wait_ge(used, used_value)
                act.activation(xT[:, 0, :, :].rearrange("p c n -> p (c n)"), E0[:, 0:D],
                               ACT.Copy).then_inc(xT_hi, 1)

            def end0(b, c):
                if c == 3:
                    normalise(0, b)
                if c == 4:
                    split_xT(b, b.after(1, 1), None, kqv_mm if b.needs(1, 0) else None, b.after(2, 0))
                if c == 6:
                    act.wait_ge(kqv_mm, b.after(2, 1))
                    if b.needs(1, 0):
                        act.wait_ge(k_placed, b.after(32, 0))
                        act.wait_ge(q_stored, b.after(16, 0))
                    act.activation(kq_hl[:, 0, :], E1[:, :], ACT.Copy).then_inc(kq_hi, 1)
                    act.wait_ge(kqv_mm, b.after(2, 2))
                    if b.needs(1, 0):
                        act.wait_ge(v_stored, b.after(16, 0))
                    act.activation(v_hl[:, 0:D], E0[:, 0:D], ACT.Copy).then_inc(v_hi, 1)

            def split_x(c):
                act.wait_ge(x_stage_in[c], 16)
                act.activation(xhl[:, c * TPC:(c + 1) * TPC, 0:D], x_stage[:, c * TPC:(c + 1) * TPC, :],
                               ACT.Copy).then_inc(x_hi, 1)

            def slot0(b, c):
                if isinstance(b.n, int) and b.number == 0:
                    split_x(c)
                    if c == 7:
                        act.wait_ge(const_in, 32)
                        for i, scale in enumerate((1.0, 1.0 / 32.0, 1.0)):
                            act.activation(w_hl[:, 0, :, i * D:(i + 1) * D], w_stage[:, :, i * D:(i + 1) * D],
                                           ACT.Copy, scale=scale).then_inc(w_hi, 1)
                chunk_hi(b, c, t0_done, mm0, T0[c % 4], hi0)
                if b.at(1).exists() and c < PIECES:
                    row_sum(b.at(1), c)
                if b.at(-1).exists():
                    end0(b.at(-1), c)

            for p in range(PIECES):
                row_sum(Blk(0, 0), p)
            for off in range(2):
                for c in range(CHUNKS):
                    slot0(Blk(0, off), c)
            with act.Fori(1, PAIRS - 1) as n:
                for off in range(2):
                    for c in range(CHUNKS):
                        slot0(Blk(n, off), c)
            for off in range(2):
                for c in range(CHUNKS):
                    slot0(Blk(PAIRS - 1, off), c)

            def probabilities(b, p):
                act.wait_ge(maxed, b.after(2, 2))
                a = a_buf[b.par][:, p * PW:(p + 1) * PW]
                act.activation(a, a, ACT.Exp, bias=mx[:, b.par, 1:2], scale=2.0,
                               accum_out=lp[:, b.par, p:p + 1]).then_inc(exped, 1)

            def end1(b, c):
                if c == 3:
                    normalise(1, b)
                if c == 6:
                    act.wait_ge(xw_mm, b.after(1, 1))
                    if b.needs(1, 0):
                        act.wait_ge(xw_stored, b.after(16, 0))
                    act.activation(xw_out[:, :], E0[:, 0:D], ACT.Copy).then_inc(xw_copied, 1)

            def slot1(b, c):
                t = b.at(-1) if c >= 1 else b.at(-2)
                if t.exists():
                    tc = (c - 1) % CHUNKS
                    chunk_hi(t, tc, t1_done, pv_done, T1[tc % 2], hi1)
                if b.at(-1).exists() and c % 2 == 0:
                    probabilities(b.at(-1), c // 2)
                if b.at(-2).exists():
                    end1(b.at(-2), c)

            def piece_hi(layer, b, p):
                act.wait_ge(a_in[b.par][p], b.landed(layer))
                if layer == 3 or b.needs(1, 0):
                    act.wait_ge(mm2, over(b, layer - 2, 4, p + 1) - 4)
                elif p == 0:
                    act.wait_ge(qk_done, 8 * NB)
                act.activation(piece_hl[:, p, 0, :], a_buf[b.par][:, p * PW:(p + 1) * PW],
                               ACT.Copy).then_inc(hi2, 1)

            for off in range(2):
                for c in range(CHUNKS):
                    if off == 0:
                        end0(Blk(0, NB - 1), c)
                    if off == 1 and c == 7:
                        act.wait_ge(w23_in, 32)
                        act.activation(w3_hl[:, 0, :, :], w3_stage[:, :, :], ACT.Copy).then_inc(w3_hi, 1)
                    slot1(Blk(0, off), c)
            with act.Fori(1, PAIRS) as n:
                for off in range(2):
                    for c in range(CHUNKS):
                        slot1(Blk(n, off), c)
            for c in range(CHUNKS):
                slot1(Blk(0, NB), c)
                if c % 2:
                    piece_hi(2, Blk(0, 0), c // 2)
            for c in range(1):
                slot1(Blk(0, NB + 1), c)

            def y_split(b):
                act.wait_ge(y_mm, b.after(1, 1))
                act.activation(yhl[:, b.rows(), 0:D], E0[:, 0:D], ACT.Copy,
                               scale=dinv[:, bass.ds(b.rows(), 1)]).then_inc(y_hi, 1)

            def body2(layer, b, has_next=True):
                prev_layer, prev = ahead(layer, b, -1)
                for p in range(PIECES):
                    if p == 1 and prev_layer == 1:
                        end1(prev, 6)
                    if has_next:
                        piece_hi(layer, b.at(1), p)
                    if p == 0 and prev_layer == 2:
                        split_xT(prev, over(prev, 2, 1, 1), None, y_mm if prev.needs(1, 0) else None, prev.after(1, 0))
                    if p == 2 and prev_layer == 2:
                        y_split(prev)
                normalise(layer, b)

            end1(Blk(0, NB - 1), 3)
            for layer in (2, 3):
                for off in range(2):
                    body2(layer, Blk(0, off))
                with act.Fori(1, PAIRS - 1) as n:
                    for off in range(2):
                        body2(layer, Blk(n, off))
                for off in range(2):
                    body2(layer, Blk(PAIRS - 1, off), has_next=(layer, off) != (3, 1))

        @block.vector
        def _(dve):
            def settled(b, i):
                if not isinstance(b.n, int):
                    dve.memset(settle[0:1, i:i + 1], 0.0)

            def count(b, p):
                dve.wait_ge(a_in[b.par][p], b.landed())
                if b.needs(1, -1):
                    dve.wait_ge(stats, b.at(-2).after(10, 1))
                if b.needs(4, p):
                    dve.wait_ge(counted, b.after(4, p))
                dve.tensor_scalar(junk_dve[:, :], a_buf[b.par][:, p * PW:(p + 1) * PW], 0.0, 0.0, ALU.is_gt,
                                  ALU.add, accum_out=part[:, b.par, 0, p:p + 1]).then_inc(counted, 1)

            def scale_of_head(b):
                dve.wait_ge(stats, b.after(10, 4))
                if b.needs(1, -1):
                    dve.wait_ge(stats, b.at(-2).after(10, 10))
                dve.tensor_scalar(rr[:, b.par, 2:3], st[:, b.par, 2:3], HEAD_EPS, None,
                                  ALU.max).then_inc(head_scale, 1)
                dve.tensor_scalar(rr[:, b.par, 3:4], st[:, b.par, 3:4], 0.0, None,
                                  ALU.is_equal).then_inc(head_scale, 1)
                dve.wait_ge(head_scale, b.after(3, 1))
                dve.reciprocal(rr[:, b.par, 0:1], rr[:, b.par, 2:3]).then_inc(head_scale, 1)

            def reciprocal_degree(b):
                dve.wait_ge(stats, b.after(10, 10))
                dve.reciprocal(rr[:, b.par, 1:2], st[:, b.par, 9:10]).then_inc(rdeg, 1)

            def head_part(b, c):
                if c == 0:
                    dve.wait_ge(head_scale, b.after(3, 3))
                if b.needs(8, c - 1):
                    dve.wait_ge(t0_done, b.after(8, c - 1))
                dve.tensor_scalar(w_mask[:, c % 2, :], a_buf[b.par][:, c * CW:(c + 1) * CW], 0.0,
                                  rr[:, b.par, 0:1], ALU.is_gt, ALU.mult).then_inc(masked, 1)

            def chunk_lo(b, c, hi_sem, t_bank, out_sem):
                dve.wait_ge(hi_sem, b.after(8, c + 1))
                dve.tensor_tensor(chunk_hl[:, c % 4, 1, :], t_bank[:, :], f32(chunk_hl[:, c % 4, 0, :]),
                                  ALU.subtract).then_inc(out_sem, 1)

            def moments(layer, b, k):
                s, steps = ln[layer], LN_STEPS[layer]
                dve.wait_ge(s, b.after(steps, k))
                dve.bn_stats(bn6[:, :], u[:, :]).then_inc(s, 1)
                dve.wait_ge(s, b.after(steps, k + 1))
                if layer > 0 or b.needs(1, 0):
                    dve.wait_ge(normed, over(b, layer, 4, 0))
                settled(b, CHUNKS)
                dve.bn_aggr(mv[:, :], bn6[:, :]).then_inc(s, 1)

            def start_end(layer, b):
                dve.wait_ge(xres_in[b.par], b.landed(layer))
                if layer > 0 or b.needs(1, 0):
                    dve.wait_ge(xn_done, over(b, layer, 1, 0))

            def add_scaled(layer, b, k, scale):
                s, steps, o = ln[layer], LN_STEPS[layer], O[b.par]
                dve.scalar_tensor_tensor(u[:, :], o[:, 0:D], scale, xres[:, b.par, :], ALU.mult,
                                         ALU.add).then_inc(s, 1)
                dve.wait_ge(s, b.after(steps, k + 1))
                dve.scalar_tensor_tensor(u[:, :], o[:, D:2 * D], scale, u[:, :], ALU.mult,
                                         ALU.add).then_inc(s, 1)

            def split_xT(t_value):
                dve.wait_ge(xT_hi, t_value)
                dve.tensor_tensor(xT[:, 1, :, :].rearrange("p c n -> p (c n)"), E0[:, 0:D],
                                  f32(xT[:, 0, :, :]).rearrange("p c n -> p (c n)"),
                                  ALU.subtract).then_inc(xT_lo, 1)

            def end0(b, c):
                if c == 2:
                    start_end(0, b)
                    dve.wait_ge(mm0, b.after(8, 8))
                    dve.wait_ge(rdeg, b.after(1, 1))
                    add_scaled(0, b, 0, rr[:, b.par, 1:2])
                    moments(0, b, 2)
                if c == 4:
                    split_xT(b.after(1, 1))
                if c == 6:
                    dve.wait_ge(kq_hi, b.after(1, 1))
                    dve.tensor_tensor(kq_hl[:, 1, :], E1[:, :], f32(kq_hl[:, 0, :]),
                                      ALU.subtract).then_inc(kq_lo, 1)
                    dve.wait_ge(v_hi, b.after(1, 1))
                    dve.tensor_tensor(v_hl[:, D:2 * D], E0[:, 0:D], f32(v_hl[:, 0:D]),
                                      ALU.subtract).then_inc(v_lo, 1)

            def split_x(c):
                dve.wait_ge(x_hi, c + 1)
                tiles = slice(c * TPC, (c + 1) * TPC)
                dve.tensor_tensor(xhl[:, tiles, D:2 * D], x_stage[:, tiles, :], f32(xhl[:, tiles, 0:D]),
                                  ALU.subtract).then_inc(x_lo, 1)

            def slot0(b, c):
                if c < CHUNKS - 1:
                    head_part(b, c + 1)
                if isinstance(b.n, int) and b.number == 0:
                    split_x(c)
                    if c == 7:
                        for i, scale in enumerate((1.0, 1.0 / 32.0, 1.0)):
                            cols = slice(i * D, (i + 1) * D)
                            dve.wait_ge(w_hi, i + 1)
                            dve.scalar_tensor_tensor(w_hl[:, 1, :, cols], w_stage[:, :, cols], scale,
                                                     f32(w_hl[:, 0, :, cols]), ALU.mult,
                                                     ALU.subtract).then_inc(w_lo, 1)
                        dve.wait_ge(bias_in, 32)
                        dve.tensor_scalar(b_stage[:, D:2 * D], b_stage[:, D:2 * D], 1.0 / 32.0, None,
                                          ALU.mult).then_inc(bias_ready, 1)
                        dve.wait_ge(bias_ready, 1)
                        dve.tensor_copy(b_r[:, :], b_stage[:, :]).then_inc(bias_ready, 1)
                        dve.wait_ge(bias_ready, 2)
                        dve.tensor_tensor(b_r[32:33, :], b_stage[32:33, :], f32(b_r[32:33, :]),
                                          ALU.subtract).then_inc(bias_ready, 1)
                chunk_lo(b, c, hi0, T0[c % 4], lo0)
                if c == 1:
                    reciprocal_degree(b)
                if b.at(1).exists() and c in (0, 1, 3, 5):
                    count(b.at(1), (0, 1, 3, 5).index(c))
                if b.at(-1).exists():
                    end0(b.at(-1), c)
                if b.at(1).exists() and c == 7:
                    scale_of_head(b.at(1))
                    head_part(b.at(1), 0)

            for p in range(PIECES):
                count(Blk(0, 0), p)
            scale_of_head(Blk(0, 0))
            head_part(Blk(0, 0), 0)
            for off in range(2):
                for c in range(CHUNKS):
                    slot0(Blk(0, off), c)
            with dve.Fori(1, PAIRS - 1) as n:
                for off in range(2):
                    for c in range(CHUNKS):
                        slot0(Blk(n, off), c)
            for off in range(2):
                for c in range(CHUNKS):
                    slot0(Blk(PAIRS - 1, off), c)

            def add_adj(b, c):
                dve.wait_ge(qk_done, b.after(8, c + 1))
                dve.wait_ge(a_in[b.par][c // 2], b.landed(1))
                a = a_buf[b.par][:, c * CW:(c + 1) * CW]
                settled(b, c)
                dve.tensor_tensor_reduce(a, S1[c % 2][:, :], a, 1.0, -3.0e38, ALU.add, ALU.max,
                                         mxp[:, b.par, c:c + 1]).then_inc(scored, 1)

            def row_max(b):
                dve.wait_ge(scored, b.after(8, 8))
                dve.tensor_reduce(mx[:, b.par, 0:1], mxp[:, b.par, :], AX.X, ALU.max).then_inc(maxed, 1)
                dve.wait_ge(maxed, b.after(2, 1))
                if b.needs(1, -1):
                    dve.wait_ge(exped, b.at(-2).after(4, 4))
                dve.tensor_scalar(mx[:, b.par, 1:2], mx[:, b.par, 0:1], -2.0, None, ALU.mult).then_inc(maxed, 1)

            def end1(b, c):
                if c == 2:
                    start_end(1, b)
                    dve.wait_ge(exped, b.after(4, 4))
                    dve.tensor_reduce(ls[:, 0:1], lp[:, b.par, :], AX.X, ALU.add).then_inc(ln[1], 1)
                    dve.wait_ge(ln[1], b.after(6, 1))
                    dve.reciprocal(ls[:, 1:2], ls[:, 0:1]).then_inc(ln[1], 1)
                    dve.wait_ge(ln[1], b.after(6, 2))
                    dve.wait_ge(pv_done, b.after(8, 8))
                    add_scaled(1, b, 2, ls[:, 1:2])
                    moments(1, b, 4)
                if c == 4:
                    dve.wait_ge(xn_done, over(b, 1, 1, 1))
                    if b.needs(1, 0):
                        dve.wait_ge(xT_done, over(b, 1, 1, 0))
                    dve.tensor_scalar(ba[:, :], xn[:, b.par, :], 0.0, None, ALU.is_gt).then_inc(bin_done, 1)
                if c == 5:
                    dve.wait_ge(xT_done, over(b, 1, 1, 1))
                    if b.needs(1, 0):
                        dve.wait_ge(xw_mm, b.after(1, 0))
                    dve.tensor_copy(baT[:, :, :].rearrange("p c n -> p (c n)"), E0[:, 0:D]).then_inc(binT_done, 1)

            def slot1(b, c):
                if b.exists():
                    add_adj(b, c)
                    if c == CHUNKS - 1:
                        row_max(b)
                t = b.at(-1) if c >= 1 else b.at(-2)
                if t.exists():
                    tc = (c - 1) % CHUNKS
                    chunk_lo(t, tc, hi1, T1[tc % 2], lo1)
                if b.at(-2).exists():
                    end1(b.at(-2), c)

            for off in range(2):
                for c in range(CHUNKS):
                    if off == 0:
                        end0(Blk(0, NB - 1), c)
                    if off == 1 and c == 7:
                        dve.wait_ge(w23_in, 32)
                        dve.tensor_scalar(w2_sign[:, :, :], w2_stage[:, :, :], 0.0, None, ALU.is_lt).then_inc(w23_ready, 1)
                        dve.wait_ge(w23_ready, 1)
                        dve.scalar_tensor_tensor(w2_sign[:, :, :], w2_stage[:, :, :], 0.0,
                                                 f32(w2_sign[:, :, :]), ALU.is_gt,
                                                 ALU.subtract).then_inc(w23_ready, 1)
                        dve.wait_ge(w3_hi, 1)
                        dve.tensor_tensor(w3_hl[:, 1, :, :], w3_stage[:, :, :], f32(w3_hl[:, 0, :, :]),
                                          ALU.subtract).then_inc(w23_ready, 1)
                    slot1(Blk(0, off), c)
            with dve.Fori(1, PAIRS) as n:
                for off in range(2):
                    for c in range(CHUNKS):
                        slot1(Blk(n, off), c)
            def piece_lo(layer, b, p):
                dve.wait_ge(hi2, over(b, layer - 2, 4, p + 1))
                dve.tensor_tensor(piece_hl[:, p, 1, :], a_buf[b.par][:, p * PW:(p + 1) * PW],
                                  f32(piece_hl[:, p, 0, :]), ALU.subtract).then_inc(lo2, 1)

            for c in range(CHUNKS):
                slot1(Blk(0, NB), c)
                if c % 2:
                    piece_lo(2, Blk(0, 0), c // 2)
            for c in range(1):
                slot1(Blk(0, NB + 1), c)

            def end2(b, stage):
                if stage == 0:
                    start_end(2, b)
                    dve.wait_ge(mm2, b.after(4, 4))
                    dve.scalar_tensor_tensor(u[:, :], O[b.par][:, 0:D], 0.0, xres[:, b.par, :], ALU.max,
                                             ALU.add).then_inc(ln[2], 1)
                    moments(2, b, 1)
                if stage == 1:
                    split_xT(over(b, 1, 1, 1))
                if stage == 2:
                    dve.wait_ge(y_hi, b.after(1, 1))
                    dve.scalar_tensor_tensor(yhl[:, b.rows(), D:2 * D], E0[:, 0:D],
                                             dinv[:, bass.ds(b.rows(), 1)], f32(yhl[:, b.rows(), 0:D]),
                                             ALU.mult, ALU.subtract).then_inc(y_lo, 1)

            def end3(b):
                s, o = ln[3], O[b.par]
                start_end(3, b)
                dve.wait_ge(mm2, over(b, 1, 4, 4))
                dve.tensor_tensor(u[:, :], o[:, 0:D], f32(yhl[:, b.rows(), 0:D]), ALU.add).then_inc(s, 1)
                dve.wait_ge(s, b.after(7, 1))
                dve.tensor_tensor(u[:, :], o[:, D:2 * D], u[:, :], ALU.add).then_inc(s, 1)
                dve.wait_ge(s, b.after(7, 2))
                dve.tensor_tensor(u[:, :], u[:, :], f32(yhl[:, b.rows(), D:2 * D]), ALU.add).then_inc(s, 1)
                dve.wait_ge(s, b.after(7, 3))
                dve.tensor_scalar(u[:, :], u[:, :], 0.0, dinv[:, bass.ds(b.rows(), 1)], ALU.max,
                                  ALU.mult).then_inc(s, 1)
                dve.wait_ge(s, b.after(7, 4))
                dve.tensor_tensor(u[:, :], u[:, :], xres[:, b.par, :], ALU.add).then_inc(s, 1)
                moments(3, b, 5)

            def body2(layer, b, has_next=True):
                prev_layer, prev = ahead(layer, b, -1)
                for p in range(PIECES):
                    if p == 0 and prev_layer == 1:
                        end1(prev, 5)
                    if p == 3:
                        if layer == 2:
                            end2(b, 0)
                        else:
                            end3(b)
                    if has_next:
                        piece_lo(layer, b.at(1), p)
                    if p in (0, 2) and prev_layer == 2:
                        end2(prev, 1 + p // 2)

            end1(Blk(0, NB - 1), 2)
            end1(Blk(0, NB - 1), 4)
            for layer in (2, 3):
                for off in range(2):
                    body2(layer, Blk(0, off))
                with dve.Fori(1, PAIRS - 1) as n:
                    for off in range(2):
                        body2(layer, Blk(n, off))
                for off in range(2):
                    body2(layer, Blk(PAIRS - 1, off), has_next=(layer, off) != (3, 1))

        @block.gpsimd
        def _(pool):
            pool.memset(f32(ones[:, :]), 1.0).then_inc(memsets, 1)
            for i, value in enumerate(CONSTANTS[:-1]):
                pool.memset(const[:, i:i + 1], value)
            pool.memset(const[:, len(CONSTANTS) - 1:], CONSTANTS[-1]).then_inc(memsets, 1)
            pool.memset(b_stage[:, :], 0.0).then_inc(memsets, 1)
            pool.wait_ge(memsets, 3)

            def row_statistics(b):
                s, q = st[:, b.par, :], part[:, b.par, :, :]

                pool.wait_ge(counted, b.after(4, 4))
                pool.wait_ge(summed, b.after(4, 4))
                if b.needs(1, -1):
                    pool.wait_ge(rdeg, b.at(-2).after(1, 1))
                pool.tensor_tensor(st[:, b.par, 12:16].rearrange("p (a c) -> p a c", a=2), q[:, :, 0:2],
                                   q[:, :, 2:4], ALU.add).then_inc(stats, 1)
                pool.wait_ge(stats, b.after(10, 1))
                pool.tensor_tensor(s[:, 0:2], s[:, 12:16:2], s[:, 13:16:2], ALU.add).then_inc(stats, 1)
                pool.wait_ge(stats, b.after(10, 2))
                pool.tensor_tensor(s[:, 2:3], s[:, 0:1], const[:, C_HALF:C_HALF + 1],
                                   ALU.pow).then_inc(stats, 1)
                pool.tensor_tensor(s[:, 3:4], s[:, 1:2], const[:, C_ONE:C_ONE + 1],
                                   ALU.add).then_inc(stats, 1)
                pool.wait_ge(head_scale, b.after(3, 3))
                pool.tensor_tensor(s[:, 5:6], s[:, 3:4], rr[:, b.par, 3:4], ALU.add).then_inc(stats, 1)
                pool.wait_ge(stats, b.after(10, 5))
                pool.tensor_tensor(s[:, 6:7], s[:, 5:6], const[:, C_MHALF:C_MHALF + 1],
                                   ALU.pow).then_inc(stats, 1)
                pool.tensor_tensor(s[:, 7:8], const[:, C_ONE:C_ONE + 1], rr[:, b.par, 3:4],
                                   ALU.subtract).then_inc(stats, 1)
                pool.wait_ge(stats, b.after(10, 7))
                pool.tensor_tensor(dinv[:, bass.ds(b.rows(), 1)], s[:, 6:7], s[:, 7:8],
                                   ALU.mult).then_inc(stats, 1)
                pool.tensor_tensor(s[:, 8:9], rr[:, b.par, 0:1], s[:, 0:1], ALU.mult).then_inc(stats, 1)
                pool.wait_ge(stats, b.after(10, 9))
                pool.tensor_tensor(s[:, 9:10], s[:, 8:9], s[:, 1:2], ALU.add).then_inc(stats, 1)

            def norm_statistics(layer, b):
                steps = LN_STEPS[layer]
                pool.wait_ge(ln[layer], b.after(steps, steps))
                if layer > 0 or b.needs(1, 0):
                    pool.wait_ge(xn_done, over(b, layer, 1, 0))
                pool.tensor_tensor(norm[:, 0:1], mv[:, 1:2], const[:, C_LN_EPS:C_LN_EPS + 1], ALU.add).then_inc(normed, 1)
                pool.wait_ge(normed, over(b, layer, 4, 1))
                pool.tensor_tensor(norm[:, 1:2], norm[:, 0:1], const[:, C_MHALF:C_MHALF + 1], ALU.pow).then_inc(normed, 1)
                pool.wait_ge(normed, over(b, layer, 4, 2))
                pool.tensor_tensor(norm[:, 3:4], mv[:, 0:1], norm[:, 1:2], ALU.mult).then_inc(normed, 1)
                pool.wait_ge(normed, over(b, layer, 4, 3))
                pool.tensor_tensor(norm[:, 2:3], const[:, C_ZERO:C_ZERO + 1], norm[:, 3:4], ALU.subtract).then_inc(normed, 1)

            row_statistics(Blk(0, 0))
            row_statistics(Blk(0, 1))
            with pool.Fori(1, PAIRS) as n:
                for off in range(2):
                    norm_statistics(0, Blk(n, off - 2))
                    row_statistics(Blk(n, off))
            for off in range(2):
                norm_statistics(0, Blk(PAIRS, off - 2))
            for layer in range(1, 4):
                with pool.Fori(0, PAIRS) as n:
                    for off in range(2):
                        norm_statistics(layer, Blk(n, off))


def kernel(x, adj, L1_gnn_Wq, L1_gnn_bq, L1_gnn_Wk, L1_gnn_bk, L1_gnn_Wv, L1_gnn_bv, L2_gnn_weight,
           L3_gnn_weight):
    import numpy as np
    import concourse.bacc as bacc
    from concourse.bass_utils import run_bass_kernel_spmd

    x, adj = np.ascontiguousarray(x), np.ascontiguousarray(adj)
    arrays = {
        "x_in": x,
        "adj": adj,
        "adjT": np.ascontiguousarray(adj.reshape(NB, P, NB, P).transpose(0, 3, 2, 1)).reshape(NB, P, N),
        "wkqv": np.ascontiguousarray(np.concatenate(
            [np.asarray(w).T for w in (L1_gnn_Wk, L1_gnn_Wq, L1_gnn_Wv)], axis=1)),
        "bias": np.concatenate([np.asarray(b) for b in (L1_gnn_bk, L1_gnn_bq, L1_gnn_bv)]).reshape(1, 3 * D),
        "w2t": np.ascontiguousarray(np.asarray(L2_gnn_weight).T),
        "w3": np.ascontiguousarray(L3_gnn_weight),
        "ident_in": np.eye(P, dtype=np.float32),
    }
    nc = bacc.Bacc("TRN2", target_bir_lowering=False, num_devices=1, dynamic_dma_scratch_size=1024)
    args = {n: nc.dram_tensor(n, a.shape, mybir.dt.from_np(a.dtype), kind="ExternalInput").ap()
            for n, a in arrays.items()}
    args["out"] = nc.dram_tensor("out", (N, D), F32, kind="ExternalOutput").ap()
    build(nc, **args)
    r = run_bass_kernel_spmd(nc, [arrays], core_ids=[0])
    return r.results[0]["out"]
```

```python
import concourse.bass as bass
from concourse import mybir
from contextlib import ExitStack

P = 128
N = 4096
D = 256
NB = N // P
CHUNKS = 8
CW = N // CHUNKS
TPC = CW // P
PIECES = 4
PW = N // PIECES
TPP = PW // P
DC = D // P
LN_EPS = 1e-5
HEAD_EPS = 1e-12
PAIRS = NB // 2
CONSTANTS = (0.5, -0.5, LN_EPS, 1.0, 0.0)
C_HALF, C_MHALF, C_LN_EPS, C_ONE, C_ZERO = range(len(CONSTANTS))

F32 = mybir.dt.float32
F32R = mybir.dt.float32r
BF16 = mybir.dt.bfloat16
U8 = mybir.dt.uint8
ALU = mybir.AluOpType
ACT = mybir.ActivationFunctionType
AX = mybir.AxisListType


class Blk:

    def __init__(self, n, off):
        self.n, self.off = n, off
        self.par = off % 2

    def at(self, shift):
        return Blk(self.n, self.off + shift)

    @property
    def number(self):
        return 2 * self.n + self.off

    def exists(self):
        return not isinstance(self.n, int) or 0 <= self.number < NB

    def after(self, per_block, k):
        return 2 * per_block * self.n + per_block * self.off + k

    def needs(self, per_block, k):
        return not isinstance(self.n, int) or self.after(per_block, k) > 0

    def landed(self, layer=0):
        return 16 * self.n + 16 * (self.off // 2 + 1 + PAIRS * layer)

    def rows(self):
        return self.number


class Pair:

    def __init__(self, n, off):
        self.n, self.off = n, off

    @property
    def number(self):
        return self.n + self.off

    def after(self, per_pair, k):
        return per_pair * self.n + per_pair * self.off + k

    def needs(self, per_pair, k):
        return not isinstance(self.n, int) or self.after(per_pair, k) > 0

    def exists(self):
        return not isinstance(self.n, int) or self.number >= 0


def build(nc, x_in, adj, adjT, wkqv, bias, w2t, w3, ident_in, out):
    ctx = ExitStack()
    with ctx:
        def sb(name, shape, dt):
            return ctx.enter_context(nc.sbuf_tensor(name, shape, dt))

        def overlay(*groups):
            made = []
            for i, group in enumerate(groups):
                stack = ctx if i == len(groups) - 1 else ExitStack()
                made += [stack.enter_context(nc.sbuf_tensor(*t)) for t in group]
                if stack is not ctx:
                    stack.close()
            return made

        def sem(name):
            return ctx.enter_context(nc.semaphore(name))

        ident = sb("ident", [P, P], F32)
        ones = sb("ones", [P, 2 * P], F32R)
        const = sb("const", [P, len(CONSTANTS)], F32)
        dinv = sb("dinv", [P, NB], F32)
        xhl, vhl, yhl = overlay([("xhl", [P, NB, 2 * D], F32R)], [("vhl", [P, NB, 2 * D], F32R)],
                                [("yhl", [P, NB, 2 * D], F32R)])
        x_stage, w_stage, b_stage, xw, piece_hl, kT = overlay(
            [("x_stage", [P, NB, D], F32), ("w_stage", [P, DC, 3 * D], F32), ("b_stage", [P, 3 * D], F32)],
            [("xw", [P, NB, D], F32R), ("piece_hl", [P, PIECES, 2, PW], F32R)],
            [("kT", [P, 2, DC, N], F32R)])
        a_buf = [sb(f"a_buf{i}", [P, N], F32) for i in range(2)]
        chunk_hl = sb("chunk_hl", [P, 4, 2, CW], F32R)
        xres = sb("xres", [P, 2, D], F32)
        u = sb("u", [P, D], F32)
        xn = sb("xn", [P, 2, D], F32)
        xT = sb("xT", [P, 2, DC, 2, P], F32R)
        settle = sb("settle", [1, CHUNKS + 1], F32)
        bn6 = sb("bn6", [P, 6], F32)
        mv = sb("mv", [P, 2], F32)
        norm = sb("norm", [P, 4], F32)
        part = sb("part", [P, 2, 2, PIECES], F32)
        st = sb("st", [P, 2, 16], F32)
        rr = sb("rr", [P, 2, 4], F32)
        qt = sb("qt", [P, 2, 2, D], F32R)
        mxp = sb("mxp", [P, 2, CHUNKS], F32)
        mx = sb("mx", [P, 2, 2], F32)
        lp = sb("lp", [P, 2, PIECES], F32)
        ls = sb("ls", [P, 2], F32)
        (w2_stage, w3_stage, w3_hl, w2_sign, ba, baT, xw_out,
         w_hl, b_r, mask, junk_act, kq_hl, v_hl) = overlay(
            [("w2_stage", [P, DC, D], F32), ("w3_stage", [P, DC, D], F32), ("w3_hl", [P, 2, DC, D], F32R),
             ("w2_sign", [P, DC, D], F32R), ("ba", [P, D], F32), ("baT", [P, DC, P], F32R),
             ("xw_out", [P, D], F32R)],
            [("w_hl", [P, 2, DC, 3 * D], F32R), ("b_r", [P, 3 * D], F32R), 
             ("mask", [P, N], U8), ("junk_act", [P, PW], BF16), ("kq_hl", [P, 2, DC, 2 * P], F32R),
             ("v_hl", [P, 2 * D], F32R)])

        banks = [ctx.enter_context(nc.psum_tensor(f"bank{i}", [P, 512], F32)) for i in range(8)]
        T0 = banks[0:4]
        S1, T1 = banks[0:2], banks[2:4]
        O = banks[4:6]
        E0, E1 = banks[6], banks[7]

        def dram(name, shape, dt):
            return nc.dram_tensor(name, shape, dt).ap()

        def f32(ap):
            return ap.bitcast(F32)

        x_mid = [dram(f"x_mid{i}", [N, D], F32) for i in range(3)]
        x_of = [x_in] + x_mid + [out]
        q_scr = dram("q_scr", [PAIRS, P, 2 * DC, 2, P], F32)
        v_scr = dram("v_scr", [NB, P, 2 * D], F32)
        xw_scr = dram("xw_scr", [NB, P, D], F32)

        def x_rows(layer, b):
            return x_of[layer].rearrange("(b p) d -> b p d", p=P)[b.rows()]

        const_in = sem("const_in")
        bias_in = sem("bias_in")
        x_stage_in = [sem(f"x_stage_in{c}") for c in range(CHUNKS)]
        a_in = [[sem(f"a_in{par}_{p}") for p in range(PIECES)] for par in range(2)]
        xres_in = [sem(f"xres_in{par}") for par in range(2)]
        x_out = [sem(f"x_out{par}") for par in range(2)]
        k_placed, q_stored, v_stored = sem("k_placed"), sem("q_stored"), sem("v_stored")
        q_in = [sem(f"q_in{par}") for par in range(2)]
        v_in = [sem(f"v_in{c}") for c in range(CHUNKS)]
        w23_in = sem("w23_in")
        xw_stored = sem("xw_stored")
        xw_in = sem("xw_in")
        memsets = sem("memsets")
        x_hi, x_lo = sem("x_hi"), sem("x_lo")
        w_hi, w_lo = sem("w_hi"), sem("w_lo")
        bias_ready = sem("bias_ready")
        w23_ready, w3_hi = sem("w23_ready"), sem("w3_hi")
        counted = sem("counted")
        summed = sem("summed")
        stats = sem("stats")
        head_scale = sem("head_scale")
        rdeg = sem("rdeg")
        inc_done = sem("inc_done")
        t0_done = sem("t0_done")
        hi0, lo0 = sem("hi0"), sem("lo0")
        mm0 = sem("mm0")
        v_mm, v_hi, v_lo = sem("v_mm"), sem("v_hi"), sem("v_lo")
        o_scaled = sem("o_scaled")
        o_plus_x = sem("o_plus_x")
        kq_mm, kq_hi, kq_lo = sem("kq_mm"), sem("kq_hi"), sem("kq_lo")
        qk_done = sem("qk_done")
        scored = sem("scored")
        maxed = sem("maxed")
        exped = sem("exped")
        t1_done = sem("t1_done")
        hi1, lo1 = sem("hi1"), sem("lo1")
        pv_done = sem("pv_done")
        bin_done, binT_done = sem("bin_done"), sem("binT_done")
        xw_mm, xw_copied = sem("xw_mm"), sem("xw_copied")
        hi2, lo2, mm2 = sem("hi2"), sem("lo2"), sem("mm2")
        y_mm, y_hi, y_lo = sem("y_mm"), sem("y_hi"), sem("y_lo")
        LN_STEPS = [3, 6, 3, 7]
        ln = [sem(f"ln{i}") for i in range(4)]
        normed = sem("normed")
        xn_done = sem("xn_done")
        xT_done = sem("xT_done")
        xT_hi, xT_lo = sem("xT_hi"), sem("xT_lo")

        block = ctx.enter_context(nc.Block())

        def ahead(layer, b, k):
            if not isinstance(b.n, int):
                return layer, b.at(k)
            return layer + (b.number + k) // NB, Blk(0, (b.number + k) % NB)

        def over(b, layer, per_block, k):
            return b.after(per_block, k) + per_block * NB * layer

        @block.sync
        def _(sp):
            def load_a(layer, b, p):
                sp.dma_start(a_buf[b.par][:, p * PW:(p + 1) * PW],
                             (adj.rearrange("(b p) n -> b p n", p=P) if layer < 2 else adjT)[b.rows()]
                             [:, p * PW:(p + 1) * PW]).then_inc(a_in[b.par][p], 16)

            def load_xres(layer, b):
                if layer > 0:
                    sp.wait_ge(x_out[b.par], 16 * PAIRS * layer)
                sp.dma_start(xres[:, b.par, :], x_rows(layer, b)).then_inc(xres_in[b.par], 16)

            def store_x(layer, b):
                sp.wait_ge(xn_done, over(b, layer, 1, 1))
                sp.dma_start(x_rows(layer + 1, b), xn[:, b.par, :]).then_inc(x_out[b.par], 16)

            def read0(b, p):
                sp.wait_ge(t0_done, b.after(8, 2 * p + 2))

            def store_k(m):
                sp.wait_ge(kq_hi, m.after(2, 1))
                sp.wait_ge(kq_lo, m.after(2, 1))
                for h in range(2):
                    sp.dma_start(f32(kT[:, h, :, bass.ds(m.number * 2 * P, 2 * P)]),
                                 f32(kq_hl[:, h, :, :])).then_inc(k_placed, 16)

            def store_q(m):
                sp.wait_ge(kq_hi, m.after(2, 2))
                sp.wait_ge(kq_lo, m.after(2, 2))
                sp.dma_start(q_scr[m.number].rearrange("p c b i -> p (c b i)"),
                             f32(kq_hl[:, :, :, :]).rearrange("p h c n -> p (h c n)")).then_inc(q_stored, 16)

            def store_v(b):
                sp.wait_ge(v_lo, b.after(1, 1))
                sp.dma_start(v_scr[b.rows()], f32(v_hl[:, :])).then_inc(v_stored, 16)

            def body0(b, layer, nxt):
                pair = Pair(b.n, -1)
                if b.needs(1, -1):
                    sp.wait_ge(ln[0], b.at(-2).after(3, 1))
                load_xres(0, b)
                read0(b, 0)
                load_a(layer, nxt, 0)
                if b.at(-2).exists():
                    store_v(b.at(-2))
                read0(b, 1)
                load_a(layer, nxt, 1)
                if b.par and pair.exists():
                    store_k(pair)
                read0(b, 2)
                load_a(layer, nxt, 2)
                if b.at(-1).exists():
                    store_x(0, b.at(-1))
                if b.par and pair.exists():
                    store_q(pair)
                read0(b, 3)
                load_a(layer, nxt, 3)

            first, second = Blk(0, 0), Blk(0, 1)
            sp.dma_start(a_buf[0][:, 0:PW], adj[0:P, 0:PW]).then_inc(a_in[0][0], 16)

            def load_x_stage(c):
                tiles = slice(c * TPC, (c + 1) * TPC)
                sp.dma_start(x_stage[:, tiles, :], x_in.rearrange("(t p) d -> p t d", p=P)[:, tiles, :]
                             ).then_inc(x_stage_in[c], 16)

            load_x_stage(0)
            sp.dma_start(ident[:, :], ident_in).then_inc(const_in, 16)
            for p in range(1, PIECES):
                load_a(0, first, p)
            load_x_stage(1)
            load_x_stage(2)
            load_a(0, second, 0)
            load_x_stage(3)
            load_x_stage(4)
            load_a(0, second, 1)
            load_a(0, second, 2)
            load_x_stage(5)
            load_x_stage(6)
            load_a(0, second, 3)
            load_x_stage(7)
            sp.dma_start(w_stage[:, :, :], wkqv.rearrange("(c p) n -> p c n", p=P)).then_inc(const_in, 16)
            sp.wait_ge(memsets, 3)
            sp.dma_start(b_stage[0:1, :], bias).then_inc(bias_in, 16)
            sp.dma_start(b_stage[32:33, :], bias).then_inc(bias_in, 16)

            for off in range(2):
                body0(Blk(0, off), 0, Blk(0, off + 2))
            with sp.Fori(1, PAIRS - 1) as n:
                for off in range(2):
                    body0(Blk(n, off), 0, Blk(n, off + 2))
            def load_q(b):
                sp.dma_start(f32(qt[:, b.par, :, :]).rearrange("p h (c i) -> p (h c) i", c=DC),
                             q_scr[b.n + b.off // 2][:, :, b.par, :]).then_inc(q_in[b.par], 16)

            sp.wait_ge(q_stored, 16 * (PAIRS - 2))
            for off in range(2):
                load_q(Blk(0, off))
            for off in range(2):
                body0(Blk(PAIRS - 1, off), 1, Blk(0, off))

            def store_xw(b):
                sp.wait_ge(xw_copied, b.after(1, 1))
                sp.dma_start(xw_scr[b.rows()], f32(xw_out[:, :])).then_inc(xw_stored, 16)

            def body1(b, nxt, layer):
                if b.at(-2).exists():
                    sp.wait_ge(t1_done, b.at(-2).after(8, 8))
                    load_a(1, b, 3)
                if b.needs(1, 0):
                    sp.wait_ge(qk_done, b.at(-1).after(8, 8))
                if not isinstance(b.n, int) or b.number > 0:
                    sp.wait_ge(q_stored, 16 * PAIRS)
                    load_q(nxt)
                for p in range(3):
                    if b.at(-1).exists():
                        sp.wait_ge(t1_done, b.at(-1).after(8, 2 * p + 2))
                        load_a(layer, nxt, p)
                    if p == 0:
                        if b.at(-2).exists():
                            store_x(1, b.at(-2))
                            sp.wait_ge(ln[1], b.at(-2).after(6, 4))
                        else:
                            sp.wait_ge(ln[0], 3 * (NB - 2 + b.number) + 1)
                        load_xres(1, b)
                if b.at(-2).exists():
                    store_xw(b.at(-2))

            def load_v(c):
                sp.dma_start(f32(vhl[:, c * TPC:(c + 1) * TPC, :]),
                             v_scr.rearrange("b p n -> p b n")[:, c * TPC:(c + 1) * TPC, :]).then_inc(v_in[c], 16)

            store_v(Blk(0, NB - 2))
            sp.wait_ge(mm0, 8 * NB)
            sp.wait_ge(v_stored, 16 * (NB - 1))
            for c in range(3):
                load_v(c)
            store_x(0, Blk(0, NB - 1))
            store_k(Pair(0, PAIRS - 1))
            store_v(Blk(0, NB - 1))
            load_v(3)
            load_v(4)
            body1(Blk(0, 0), Blk(0, 1), 1)
            store_q(Pair(0, PAIRS - 1))
            load_v(5)
            load_v(6)
            sp.wait_ge(v_stored, 16 * NB)
            load_v(7)
            sp.wait_ge(k_placed, 32 * PAIRS)
            sp.wait_ge(q_stored, 16 * PAIRS)
            sp.wait_ge(v_mm, NB)
            sp.dma_start(w2_stage[:, :, :], w2t.rearrange("(c p) n -> p c n", p=P)).then_inc(w23_in, 16)
            sp.dma_start(w3_stage[:, :, :], w3.rearrange("(c p) n -> p c n", p=P)).then_inc(w23_in, 16)
            body1(Blk(0, 1), Blk(0, 2), 1)
            with sp.Fori(1, PAIRS - 1) as n:
                for off in range(2):
                    body1(Blk(n, off), Blk(n, off + 1), 1)
            body1(Blk(PAIRS - 1, 0), Blk(PAIRS - 1, 1), 1)
            last = Blk(0, NB - 1)
            sp.wait_ge(t1_done, last.at(-2).after(8, 8))
            load_a(1, last, 3)
            for p in range(PIECES):
                sp.wait_ge(t1_done, last.at(-1).after(8, 2 * p + 2))
                load_a(2, Blk(0, 0), p)
                if p == 0:
                    store_x(1, last.at(-2))
                    sp.wait_ge(ln[1], last.at(-2).after(6, 4))
                    load_xres(1, last)
                if p == 2:
                    store_xw(last.at(-2))
            sp.wait_ge(qk_done, 8 * NB)
            sp.wait_ge(xw_stored, 16 * (NB - 2))
            sp.dma_start(f32(xw[:, 0:NB - 2, :]), xw_scr.rearrange("b p n -> p b n")[:, 0:NB - 2, :]).then_inc(xw_in, 16)
            store_x(1, last.at(-1))
            sp.wait_ge(ln[1], last.at(-1).after(6, 4))
            load_xres(2, Blk(0, 0))
            sp.wait_ge(xw_copied, NB - 1)
            sp.dma_start(f32(xw[:, NB - 2, :]), f32(xw_out[:, :])).then_inc(xw_stored, 16)
            for p in range(PIECES):
                sp.wait_ge(t1_done, last.after(8, 2 * p + 2))
                load_a(2, Blk(0, 1), p)
            for p in range(PIECES):
                sp.wait_ge(lo2, p + 1)
                load_a(2, Blk(0, 2), p)

            def body2(layer, b):
                for p in range(PIECES):
                    to_layer, to = ahead(layer, b, 3)
                    if to_layer < 4:
                        sp.wait_ge(lo2, over(b.at(1), layer - 2, 4, p + 1))
                        load_a(to_layer, to, p)
                    if p == 0:
                        prev_layer, prev = ahead(layer, b, -1)
                        store_x(prev_layer, prev)
                        if (prev_layer, layer) == (1, 2):
                            sp.wait_ge(xw_copied, NB)
                            sp.dma_start(f32(xw[:, NB - 1, :]), f32(xw_out[:, :])).then_inc(xw_stored, 16)
                        to_layer, to = ahead(layer, b, 1)
                        if to_layer < 4:
                            steps = LN_STEPS[prev_layer]
                            sp.wait_ge(ln[prev_layer], prev.after(steps, steps - 2))
                            load_xres(to_layer, to)

            for layer in (2, 3):
                for off in range(2):
                    body2(layer, Blk(0, off))
                with sp.Fori(1, PAIRS - 2) as n:
                    for off in range(2):
                        body2(layer, Blk(n, off))
                for off in range(4):
                    body2(layer, Blk(PAIRS - 2, off))
            store_x(3, last)
            for par in range(2):
                sp.wait_ge(x_out[par], 16 * PAIRS * 4)
            sp.wait_ge(xw_stored, 16 * NB)

        @block.tensor
        def _(pe):
            def transpose0(b, c):
                pe.wait_ge(inc_done, b.after(8, c + 1))
                if b.needs(8, c - 3):
                    pe.wait_ge(lo0, b.after(8, c - 3))
                for t in range(TPC):
                    cols = slice(t * P, (t + 1) * P)
                    mm = pe.transpose(T0[c % 4][:, cols], a_buf[b.par][:, c * CW + t * P:c * CW + (t + 1) * P], ident[:, :])
                mm.then_inc(t0_done, 1)

            def by_hi_lo(b, c, values, done):
                o = O[b.par]
                for t in range(TPC):
                    j = c * TPC + t
                    hi = chunk_hl[:, c % 4, 0, t * P:(t + 1) * P]
                    lo = chunk_hl[:, c % 4, 1, t * P:(t + 1) * P]
                    if j < NB - 1:
                        pe.matmul(o[:, :], hi, values[:, j, :], start=(j == 0), stop=False)
                        mm = pe.matmul(o[:, D:2 * D], lo, values[:, j, 0:D], start=False, stop=False)
                    else:
                        pe.matmul(o[:, D:2 * D], lo, values[:, j, 0:D], start=False, stop=False)
                        mm = pe.matmul(o[:, :], hi, values[:, j, :], start=False, stop=True)
                mm.then_inc(done, 1)

            def products0(b, c):
                pe.wait_ge(lo0, b.after(8, c + 1))
                if isinstance(b.n, int) and b.number == 0:
                    pe.wait_ge(x_lo, c + 1)
                if c == 0 and b.needs(1, -1):
                    pe.wait_ge(ln[0], b.at(-2).after(3, 1))
                by_hi_lo(b, c, xhl, mm0)

            def block_transpose(layer, b, src, ready, value):
                pe.wait_ge(ready, value)
                for dc in range(DC):
                    mm = pe.transpose(E0[:, dc * P:(dc + 1) * P], src[:, dc * P:(dc + 1) * P], ident[:, :])
                mm.then_inc(xT_done, 1)

            def end0_transpose(b):
                if b.needs(1, 0):
                    pe.wait_ge(v_lo, b.after(1, 0))
                block_transpose(0, b, xn[:, b.par, :], xn_done, b.after(1, 1))

            def end0_v(b):
                pe.wait_ge(xT_hi, b.after(1, 1))
                pe.wait_ge(xT_lo, b.after(1, 1))
                if isinstance(b.n, int) and b.number == 0:
                    pe.wait_ge(w_lo, 1)
                    pe.wait_ge(bias_ready, 1)
                v = slice(2 * D, 3 * D)
                x_hi, x_lo = xT[:, 0, :, b.par, :], xT[:, 1, :, b.par, :]
                pe.matmul(E0[:, 0:D], ones[:, 0:P], b_r[:, v], start=True, stop=False)
                for dc in range(DC):
                    pe.matmul(E0[:, 0:D], x_lo[:, dc, :], w_hl[:, 0, dc, v], start=False, stop=False)
                    pe.matmul(E0[:, 0:D], x_hi[:, dc, :], w_hl[:, 1, dc, v], start=False, stop=False)
                    mm = pe.matmul(E0[:, 0:D], x_hi[:, dc, :], w_hl[:, 0, dc, v],
                                   start=False, stop=(dc == DC - 1))
                mm.then_inc(v_mm, 1)

            def end0_kq(m, which):
                for g in range(DC):
                    end0_kq_half(m, which, g)

            def end0_kq_half(m, which, g):
                if g == 0:
                    if m.needs(2, which):
                        pe.wait_ge(kq_lo, m.after(2, which))
                    if which == 0:
                        pe.wait_ge(xT_hi, m.after(2, 2))
                        pe.wait_ge(xT_lo, m.after(2, 2))
                out_cols = slice(g * 2 * P, (g + 1) * 2 * P)
                cols = slice((which * DC + g) * P, (which * DC + g + 1) * P)
                pe.matmul(E1[:, out_cols], b_r[:, cols], ones[:, :], start=True, stop=False)
                for dc in range(DC):
                    x_hi = xT[:, 0, dc, :, :].rearrange("p b i -> p (b i)")
                    x_lo = xT[:, 1, dc, :, :].rearrange("p b i -> p (b i)")
                    pe.matmul(E1[:, out_cols], w_hl[:, 1, dc, cols], x_hi, start=False, stop=False)
                    pe.matmul(E1[:, out_cols], w_hl[:, 0, dc, cols], x_lo, start=False, stop=False)
                    mm = pe.matmul(E1[:, out_cols], w_hl[:, 0, dc, cols], x_hi,
                                   start=False, stop=(dc == DC - 1))
                if g == DC - 1:
                    mm.then_inc(kq_mm, 1)

            def slot0(b, c):
                if b.exists():
                    transpose0(b, c)
                prev = b if c >= 3 else b.at(-1)
                if prev.exists():
                    products0(prev, (c - 3) % CHUNKS)
                if b.at(-1).exists() and c == 7:
                    end0_transpose(b.at(-1))
                if b.at(-2).exists() and c == 0:
                    end0_v(b.at(-2))
                if b.par and Pair(b.n, -1).exists() and c in (1, 2, 4, 5):
                    end0_kq_half(Pair(b.n, -1), c // 4, (c - 1) % 3)

            pe.wait_ge(const_in, 16)
            pe.wait_ge(memsets, 1)
            for off in range(2):
                for c in range(CHUNKS):
                    slot0(Blk(0, off), c)
            with pe.Fori(1, PAIRS) as n:
                for off in range(2):
                    for c in range(CHUNKS):
                        slot0(Blk(n, off), c)

            def scores(b, c):
                s = S1[c % 2]
                if c == 0:
                    pe.wait_ge(q_in[b.par], b.landed())
                if isinstance(b.n, int) and b.number == 0:
                    pe.wait_ge(k_placed, 32 * (PAIRS if c == CHUNKS - 1 else PAIRS - 1))
                    if c == 0:
                        pe.wait_ge(lo0, 8 * NB)
                if b.needs(8, c - 1):
                    pe.wait_ge(scored, b.after(8, c - 1))
                q = qt[:, b.par, :, :]
                cols = slice(c * CW, (c + 1) * CW)
                for dc in range(DC):
                    dd = slice(dc * P, (dc + 1) * P)
                    pe.matmul(s[:, :], q[:, 1, dd], kT[:, 0, dc, cols], start=(dc == 0), stop=False)
                    pe.matmul(s[:, :], q[:, 0, dd], kT[:, 1, dc, cols], start=False, stop=False)
                    mm = pe.matmul(s[:, :], q[:, 0, dd], kT[:, 0, dc, cols], start=False, stop=(dc == DC - 1))
                mm.then_inc(qk_done, 1)

            def transpose1(b, c):
                pe.wait_ge(exped, b.after(4, c // 2 + 1))
                if b.needs(8, c - 1):
                    pe.wait_ge(lo1, b.after(8, c - 1))
                for t in range(TPC):
                    mm = pe.transpose(T1[c % 2][:, t * P:(t + 1) * P],
                                      a_buf[b.par][:, c * CW + t * P:c * CW + (t + 1) * P], ident[:, :])
                mm.then_inc(t1_done, 1)

            def products1(b, c):
                pe.wait_ge(lo1, b.after(8, c + 1))
                if isinstance(b.n, int) and b.number == 0:
                    pe.wait_ge(v_in[c], 16)
                    if c == 0:
                        pe.wait_ge(ln[0], 3 * NB)
                by_hi_lo(b, c, vhl, pv_done)

            def end1_transpose(b):
                if b.needs(1, 0):
                    pe.wait_ge(xw_copied, b.after(1, 0))
                block_transpose(1, b, ba, bin_done, b.after(1, 1))

            def end1_xw(b):
                pe.wait_ge(binT_done, b.after(1, 1))
                if isinstance(b.n, int) and b.number == 0:
                    pe.wait_ge(w23_ready, 2)
                for dc in range(DC):
                    mm = pe.matmul(E0[:, 0:D], baT[:, dc, :], w2_sign[:, dc, :], start=(dc == 0), stop=(dc == 1))
                mm.then_inc(xw_mm, 1)

            def slot1(b, c):
                if b.exists():
                    scores(b, c)
                t = b.at(-1) if c >= 1 else b.at(-2)
                if t.exists():
                    transpose1(t, (c - 1) % CHUNKS)
                m = b.at(-1) if c >= 2 else b.at(-2)
                if m.exists():
                    products1(m, (c - 2) % CHUNKS)
                if b.at(-2).exists():
                    if c == 5:
                        end1_transpose(b.at(-2))
                    if c == 6:
                        end1_xw(b.at(-2))

            for off in range(2):
                for c in range(CHUNKS):
                    if off == 0:
                        if c == 0:
                            end0_v(Blk(0, NB - 2))
                            for last_chunk in range(5, CHUNKS):
                                products0(Blk(0, NB - 1), last_chunk)
                    slot1(Blk(0, off), c)
                    if off == 0:
                        if c == 2:
                            end0_transpose(Blk(0, NB - 1))
                        if c == 3:
                            end0_kq(Pair(0, PAIRS - 1), 0)
                            end0_v(Blk(0, NB - 1))
                        if c == 4:
                            end0_kq(Pair(0, PAIRS - 1), 1)
            with pe.Fori(1, PAIRS) as n:
                for off in range(2):
                    for c in range(CHUNKS):
                        slot1(Blk(n, off), c)
            for c in range(CHUNKS):
                slot1(Blk(0, NB), c)
            for c in range(2):
                slot1(Blk(0, NB + 1), c)

            def products2(layer, b, p):
                pe.wait_ge(lo2, over(b, layer - 2, 4, p + 1))
                if layer == 2 and isinstance(b.n, int) and b.number == 0:
                    if p == 0:
                        pe.wait_ge(xw_in, 16)
                    if p == PIECES - 1:
                        pe.wait_ge(xw_stored, 16 * NB)
                if layer == 3 and isinstance(b.n, int) and b.number == 0:
                    pe.wait_ge(y_lo, NB if p == PIECES - 1 else NB - 1)
                if p == 0:
                    before = b.at(-2)
                    if b.needs(1, -1):
                        pe.wait_ge(ln[layer], before.after(LN_STEPS[layer], LN_STEPS[layer] - 2))
                    else:
                        pe.wait_ge(ln[layer - 1], LN_STEPS[layer - 1] * (NB + b.number - 1) - 2)
                o = O[b.par]
                for t in range(TPP):
                    j = p * TPP + t
                    hi = piece_hl[:, p, 0, t * P:(t + 1) * P]
                    lo = piece_hl[:, p, 1, t * P:(t + 1) * P]
                    if layer == 2:
                        pe.matmul(o[:, 0:D], hi, xw[:, j, :], start=(j == 0), stop=False)
                        mm = pe.matmul(o[:, 0:D], lo, xw[:, j, :], start=False, stop=(j == NB - 1))
                    elif j < NB - 1:
                        pe.matmul(o[:, :], hi, yhl[:, j, :], start=(j == 0), stop=False)
                        mm = pe.matmul(o[:, D:2 * D], lo, yhl[:, j, 0:D], start=False, stop=False)
                    else:
                        pe.matmul(o[:, D:2 * D], lo, yhl[:, j, 0:D], start=False, stop=False)
                        mm = pe.matmul(o[:, :], hi, yhl[:, j, :], start=False, stop=True)
                mm.then_inc(mm2, 1)

            def end2_transpose(b):
                if b.needs(1, 0):
                    pe.wait_ge(y_lo, b.after(1, 0))
                else:
                    pe.wait_ge(xw_copied, NB)
                block_transpose(2, b, xn[:, b.par, :], xn_done, over(b, 2, 1, 1))

            def end2_y(b):
                pe.wait_ge(xT_hi, over(b, 1, 1, 1))
                pe.wait_ge(xT_lo, over(b, 1, 1, 1))
                x_hi, x_lo = xT[:, 0, :, b.par, :], xT[:, 1, :, b.par, :]
                for dc in range(DC):
                    pe.matmul(E0[:, 0:D], x_lo[:, dc, :], w3_hl[:, 0, dc, :], start=(dc == 0), stop=False)
                    pe.matmul(E0[:, 0:D], x_hi[:, dc, :], w3_hl[:, 1, dc, :], start=False, stop=False)
                    mm = pe.matmul(E0[:, 0:D], x_hi[:, dc, :], w3_hl[:, 0, dc, :],
                                   start=False, stop=(dc == DC - 1))
                mm.then_inc(y_mm, 1)

            def body2(layer, b):
                prev_layer, prev = ahead(layer, b, -1)
                for p in range(PIECES):
                    products2(layer, b, p)
                    if prev_layer == 1:
                        if p < 2:
                            (end1_transpose, end1_xw)[p](prev)
                    elif prev_layer == 2:
                        if p == 1:
                            end2_transpose(prev)
                        if p == (3 if layer == 2 else 2):
                            end2_y(prev)

            for layer in (2, 3):
                for off in range(2):
                    body2(layer, Blk(0, off))
                with pe.Fori(1, PAIRS) as n:
                    for off in range(2):
                        body2(layer, Blk(n, off))

        @block.scalar
        def _(act):
            def row_sum(b, p):
                act.wait_ge(a_in[b.par][p], b.landed())
                if b.needs(1, -1):
                    act.wait_ge(stats, b.at(-2).after(10, 1))
                if b.needs(4, p):
                    act.wait_ge(summed, b.after(4, p))
                act.activation(junk_act[:, :], a_buf[b.par][:, p * PW:(p + 1) * PW], ACT.Copy,
                               accum_out=part[:, b.par, 1, p:p + 1]).then_inc(summed, 1)

            def chunk_hi(b, c, transposed, used, t_bank, out_sem):
                act.wait_ge(transposed, b.after(8, c + 1))
                if b.needs(8, c - 3):
                    act.wait_ge(used, b.after(8, c - 3))
                act.activation(chunk_hl[:, c % 4, 0, :], t_bank[:, :], ACT.Copy).then_inc(out_sem, 1)

            def normalise(layer, b):
                act.wait_ge(normed, over(b, layer, 4, 4))
                if layer > 0:
                    act.wait_ge(x_out[b.par], b.at(-2).landed(layer))
                act.activation(xn[:, b.par, :], u[:, :], ACT.Identity, bias=norm[:, 2:3],
                               scale=norm[:, 1:2]).then_inc(xn_done, 1)

            def split_xT(b, t_value, used, used_value):
                act.wait_ge(xT_done, t_value)
                if used is not None:
                    act.wait_ge(used, used_value)
                act.activation(xT[:, 0, :, b.par, :], E0[:, 0:D].rearrange("p (c i) -> p c i", c=DC),
                               ACT.Copy).then_inc(xT_hi, 1)

            def end0_scale(b):
                act.wait_ge(mm0, b.after(8, 8))
                act.wait_ge(rdeg, b.after(1, 1))
                if b.needs(1, -1):
                    act.wait_ge(x_out[b.par], b.at(-2).landed())
                    act.wait_ge(xT_done, b.at(-2).after(1, 1))
                act.activation(xn[:, b.par, :], O[b.par][:, 0:D], ACT.Copy,
                               scale=rr[:, b.par, 1:2]).then_inc(o_scaled, 1)

            def end0_xT(b):
                m = Pair(b.n, b.off // 2 - 1)
                split_xT(b, b.after(1, 1), kq_mm if m.exists() else None, m.after(2, 2))

            def end0_v(b):
                act.wait_ge(v_mm, b.after(1, 1))
                if b.needs(1, 0):
                    act.wait_ge(v_stored, b.after(16, 0))
                act.activation(v_hl[:, 0:D], E0[:, 0:D], ACT.Copy).then_inc(v_hi, 1)

            def end0_kq(m, which):
                act.wait_ge(kq_mm, m.after(2, which + 1))
                if which:
                    act.wait_ge(k_placed, m.after(32, 32))
                elif m.needs(1, 0):
                    act.wait_ge(q_stored, m.after(16, 0))
                act.activation(kq_hl[:, 0, :, :].rearrange("p c n -> p (c n)"), E1[:, :],
                               ACT.Copy).then_inc(kq_hi, 1)

            def split_x(c):
                act.wait_ge(x_stage_in[c], 16)
                act.activation(xhl[:, c * TPC:(c + 1) * TPC, 0:D], x_stage[:, c * TPC:(c + 1) * TPC, :],
                               ACT.Copy).then_inc(x_hi, 1)

            def split_weights():
                act.wait_ge(const_in, 32)
                act.wait_ge(bias_in, 32)
                act.activation(w_stage[:, :, D:2 * D], w_stage[:, :, D:2 * D], ACT.Copy,
                               scale=1.0 / 32.0).then_inc(w_hi, 1)
                act.activation(b_stage[:, D:2 * D], b_stage[:, D:2 * D], ACT.Copy,
                               scale=1.0 / 32.0).then_inc(w_hi, 1)
                act.wait_ge(w_hi, 2)
                act.activation(w_hl[:, 0, :, :], w_stage[:, :, :], ACT.Copy).then_inc(w_hi, 1)
                act.activation(b_r[:, :], b_stage[:, :], ACT.Copy).then_inc(w_hi, 1)

            def slot0(b, c):
                start = isinstance(b.n, int) and b.number == 0
                chunk_hi(b, c, t0_done, mm0, T0[c % 4], hi0)
                if start and c < CHUNKS - 1:
                    split_x(c + 1)
                if start and c == CHUNKS - 1:
                    split_weights()
                if b.at(-2).exists() and c == 1:
                    end0_v(b.at(-2))
                if b.par and Pair(b.n, -1).exists() and c in (3, 6):
                    end0_kq(Pair(b.n, -1), c // 6)
                slots = (0, 2, 3, 5) if start else (0, 1, 2, 3)
                if b.at(1).exists() and c in slots:
                    row_sum(b.at(1), slots.index(c))
                if b.at(-1).exists():
                    if c == 3:
                        end0_scale(b.at(-1))
                    if c == 6:
                        normalise(0, b.at(-1))
                    if c == 7:
                        end0_xT(b.at(-1))

            for p in range(PIECES):
                row_sum(Blk(0, 0), p)
            split_x(0)
            for off in range(2):
                for c in range(CHUNKS):
                    slot0(Blk(0, off), c)
            with act.Fori(1, PAIRS - 1) as n:
                for off in range(2):
                    for c in range(CHUNKS):
                        slot0(Blk(n, off), c)
            for off in range(2):
                for c in range(CHUNKS):
                    slot0(Blk(PAIRS - 1, off), c)

            def probabilities(b, p):
                act.wait_ge(maxed, b.after(2, 2))
                a = a_buf[b.par][:, p * PW:(p + 1) * PW]
                act.activation(a, a, ACT.Exp, bias=mx[:, b.par, 1:2], scale=2.0,
                               accum_out=lp[:, b.par, p:p + 1]).then_inc(exped, 1)

            def end1(b, c):
                if c == 3:
                    normalise(1, b)
                if c == 6:
                    act.wait_ge(xw_mm, b.after(1, 1))
                    if b.needs(1, 0):
                        act.wait_ge(xw_stored, b.after(16, 0))
                    act.activation(xw_out[:, :], E0[:, 0:D], ACT.Copy).then_inc(xw_copied, 1)

            def slot1(b, c):
                t = b.at(-1) if c >= 1 else b.at(-2)
                if t.exists():
                    tc = (c - 1) % CHUNKS
                    chunk_hi(t, tc, t1_done, pv_done, T1[tc % 2], hi1)
                if b.at(-1).exists() and c % 2 == 0:
                    probabilities(b.at(-1), c // 2)
                if b.at(-2).exists():
                    end1(b.at(-2), c)

            def piece_hi(layer, b, p):
                act.wait_ge(a_in[b.par][p], b.landed(layer))
                if layer == 3 or b.needs(1, 0):
                    act.wait_ge(mm2, over(b, layer - 2, 4, p + 1) - 4)
                elif p == 0:
                    act.wait_ge(qk_done, 8 * NB)
                act.activation(piece_hl[:, p, 0, :], a_buf[b.par][:, p * PW:(p + 1) * PW],
                               ACT.Copy).then_inc(hi2, 1)

            for off in range(2):
                for c in range(CHUNKS):
                    if off == 0:
                        if c == 0:
                            end0_v(Blk(0, NB - 2))
                            end0_scale(Blk(0, NB - 1))
                            normalise(0, Blk(0, NB - 1))
                        if c == 2:
                            end0_xT(Blk(0, NB - 1))
                        if c == 3:
                            end0_kq(Pair(0, PAIRS - 1), 0)
                            end0_v(Blk(0, NB - 1))
                        if c == 6:
                            end0_kq(Pair(0, PAIRS - 1), 1)
                    if off == 1 and c == 7:
                        act.wait_ge(w23_in, 32)
                        act.activation(w3_hl[:, 0, :, :], w3_stage[:, :, :], ACT.Copy).then_inc(w3_hi, 1)
                    slot1(Blk(0, off), c)
            with act.Fori(1, PAIRS) as n:
                for off in range(2):
                    for c in range(CHUNKS):
                        slot1(Blk(n, off), c)
            for c in range(CHUNKS):
                slot1(Blk(0, NB), c)
                if c % 2:
                    piece_hi(2, Blk(0, 0), c // 2)
            for c in range(1):
                slot1(Blk(0, NB + 1), c)

            def y_split(b):
                act.wait_ge(y_mm, b.after(1, 1))
                act.activation(yhl[:, b.rows(), 0:D], E0[:, 0:D], ACT.Copy,
                               scale=dinv[:, bass.ds(b.rows(), 1)]).then_inc(y_hi, 1)

            def body2(layer, b, has_next=True):
                prev_layer, prev = ahead(layer, b, -1)
                for p in range(PIECES):
                    if p == 1 and prev_layer == 1:
                        end1(prev, 6)
                    if has_next:
                        piece_hi(layer, b.at(1), p)
                    if p == 0 and prev_layer > 1:
                        normalise(prev_layer, prev)
                    if p == 1 and prev_layer == 2:
                        split_xT(prev, over(prev, 2, 1, 1), y_mm if prev.needs(1, 0) else None, prev.after(1, 0))
                    if p == (3 if layer == 2 else 2) and prev_layer == 2:
                        y_split(prev)

            end1(Blk(0, NB - 1), 3)
            for layer in (2, 3):
                for off in range(2):
                    body2(layer, Blk(0, off))
                with act.Fori(1, PAIRS - 1) as n:
                    for off in range(2):
                        body2(layer, Blk(n, off))
                for off in range(2):
                    body2(layer, Blk(PAIRS - 1, off), has_next=(layer, off) != (3, 1))
            normalise(3, Blk(0, NB - 1))

        @block.vector
        def _(dve):
            def settled(b, i):
                if not isinstance(b.n, int):
                    dve.memset(settle[0:1, i:i + 1], 0.0)

            def count(b, p):
                dve.wait_ge(a_in[b.par][p], b.landed())
                if b.needs(1, -1):
                    dve.wait_ge(stats, b.at(-2).after(10, 1))
                if b.at(-1).exists():
                    dve.wait_ge(inc_done, b.at(-1).after(8, 2 * p + 2))
                dve.tensor_scalar(mask[:, p * PW:(p + 1) * PW], a_buf[b.par][:, p * PW:(p + 1) * PW], 0.0, 0.0, ALU.is_gt,
                                  ALU.add, accum_out=part[:, b.par, 0, p:p + 1]).then_inc(counted, 1)

            def scale_of_head(b):
                dve.wait_ge(stats, b.after(10, 4))
                if b.needs(1, -1):
                    dve.wait_ge(stats, b.at(-2).after(10, 10))
                dve.tensor_scalar(rr[:, b.par, 0:1], st[:, b.par, 2:3], HEAD_EPS, None,
                                  ALU.max).then_inc(head_scale, 1)
                dve.tensor_scalar(rr[:, b.par, 3:4], st[:, b.par, 3:4], 0.0, None,
                                  ALU.is_equal).then_inc(head_scale, 1)

            def reciprocal_degree(b):
                dve.wait_ge(stats, b.after(10, 10))
                dve.reciprocal(rr[:, b.par, 1:2], st[:, b.par, 9:10]).then_inc(rdeg, 1)

            def scaled_inc(b, c):
                if c == 0:
                    dve.wait_ge(head_scale, b.after(2, 2))
                dve.wait_ge(counted, b.after(4, c // 2 + 1))
                a = a_buf[b.par][:, c * CW:(c + 1) * CW]
                dve.scalar_tensor_tensor(a, a, rr[:, b.par, 0:1], mask[:, c * CW:(c + 1) * CW], ALU.mult,
                                         ALU.add).then_inc(inc_done, 1)

            def chunk_lo(b, c, hi_sem, t_bank, out_sem):
                dve.wait_ge(hi_sem, b.after(8, c + 1))
                dve.tensor_tensor(chunk_hl[:, c % 4, 1, :], t_bank[:, :], f32(chunk_hl[:, c % 4, 0, :]),
                                  ALU.subtract).then_inc(out_sem, 1)

            def moments(layer, b, k):
                partial_moments(layer, b, k)
                whole_moments(layer, b, k)

            def partial_moments(layer, b, k):
                dve.wait_ge(ln[layer], b.after(LN_STEPS[layer], k))
                dve.bn_stats(bn6[:, :], u[:, :]).then_inc(ln[layer], 1)

            def whole_moments(layer, b, k):
                s, steps = ln[layer], LN_STEPS[layer]
                dve.wait_ge(s, b.after(steps, k + 1))
                if layer > 0 or b.needs(1, 0):
                    dve.wait_ge(normed, over(b, layer, 4, 0))
                settled(b, CHUNKS)
                dve.bn_aggr(mv[:, :], bn6[:, :]).then_inc(s, 1)

            def start_end(layer, b):
                dve.wait_ge(xres_in[b.par], b.landed(layer))
                if layer > 0 or b.needs(1, 0):
                    dve.wait_ge(xn_done, over(b, layer, 1, 0))

            def add_scaled(layer, b, k, scale):
                s, steps, o = ln[layer], LN_STEPS[layer], O[b.par]
                dve.scalar_tensor_tensor(u[:, :], o[:, 0:D], scale, xres[:, b.par, :], ALU.mult,
                                         ALU.add).then_inc(s, 1)
                dve.wait_ge(s, b.after(steps, k + 1))
                dve.scalar_tensor_tensor(u[:, :], o[:, D:2 * D], scale, u[:, :], ALU.mult,
                                         ALU.add).then_inc(s, 1)

            def split_xT(b, t_value):
                dve.wait_ge(xT_hi, t_value)
                dve.tensor_tensor(xT[:, 1, :, b.par, :], E0[:, 0:D].rearrange("p (c i) -> p c i", c=DC),
                                  f32(xT[:, 0, :, b.par, :]), ALU.subtract).then_inc(xT_lo, 1)

            def end0_u(b):
                dve.wait_ge(o_plus_x, b.after(1, 1))
                dve.scalar_tensor_tensor(u[:, :], O[b.par][:, D:2 * D], rr[:, b.par, 1:2], u[:, :], ALU.mult,
                                         ALU.add).then_inc(ln[0], 1)

            def end0_v(b):
                dve.wait_ge(v_hi, b.after(1, 1))
                dve.tensor_tensor(v_hl[:, D:2 * D], E0[:, 0:D], f32(v_hl[:, 0:D]),
                                  ALU.subtract).then_inc(v_lo, 1)

            def end0_kq(m, which):
                dve.wait_ge(kq_hi, m.after(2, which + 1))
                dve.tensor_tensor(kq_hl[:, 1, :, :].rearrange("p c n -> p (c n)"), E1[:, :],
                                  f32(kq_hl[:, 0, :, :]).rearrange("p c n -> p (c n)"),
                                  ALU.subtract).then_inc(kq_lo, 1)

            def slot0(b, c):
                nxt, prev = b.at(1), b.at(-1)
                if c < 6:
                    scaled_inc(b, c + 2)
                if prev.exists():
                    if c == 4:
                        end0_u(prev)
                    if c == 5:
                        whole_moments(0, prev, 1)
                if c == 5 and nxt.exists():
                    count(nxt, 3)
                chunk_lo(b, c, hi0, T0[c % 4], lo0)
                if c == 1:
                    reciprocal_degree(b)
                if nxt.exists() and c in (0, 2, 3):
                    count(nxt, (0, 2, 3).index(c))
                if prev.exists():
                    if c == 4:
                        partial_moments(0, prev, 1)
                if b.at(-2).exists() and c == 1:
                    end0_v(b.at(-2))
                if b.par and Pair(b.n, -1).exists() and c in (3, 6):
                    end0_kq(Pair(b.n, -1), c // 6)
                if nxt.exists():
                    if c == 6:
                        scale_of_head(nxt)
                    if c == 7:
                        scaled_inc(nxt, 0)
                if c == 7 and prev.exists():
                    split_xT(prev, prev.after(1, 1))
                if c == 7 and nxt.exists():
                    scaled_inc(nxt, 1)

            for p in range(PIECES):
                count(Blk(0, 0), p)
            scale_of_head(Blk(0, 0))
            scaled_inc(Blk(0, 0), 0)
            scaled_inc(Blk(0, 0), 1)
            for off in range(2):
                for c in range(CHUNKS):
                    slot0(Blk(0, off), c)
            with dve.Fori(1, PAIRS - 1) as n:
                for off in range(2):
                    for c in range(CHUNKS):
                        slot0(Blk(n, off), c)
            for off in range(2):
                for c in range(CHUNKS):
                    slot0(Blk(PAIRS - 1, off), c)

            def add_adj(b, c):
                dve.wait_ge(qk_done, b.after(8, c + 1))
                dve.wait_ge(a_in[b.par][c // 2], b.landed(1))
                a = a_buf[b.par][:, c * CW:(c + 1) * CW]
                settled(b, c)
                dve.tensor_tensor_reduce(a, S1[c % 2][:, :], a, 1.0, -3.0e38, ALU.add, ALU.max,
                                         mxp[:, b.par, c:c + 1]).then_inc(scored, 1)

            def row_max(b):
                dve.wait_ge(scored, b.after(8, 8))
                dve.tensor_reduce(mx[:, b.par, 0:1], mxp[:, b.par, :], AX.X, ALU.max).then_inc(maxed, 1)
                dve.wait_ge(maxed, b.after(2, 1))
                if b.needs(1, -1):
                    dve.wait_ge(exped, b.at(-2).after(4, 4))
                dve.tensor_scalar(mx[:, b.par, 1:2], mx[:, b.par, 0:1], -2.0, None, ALU.mult).then_inc(maxed, 1)

            def end1(b, c):
                if c == 2:
                    start_end(1, b)
                    dve.wait_ge(exped, b.after(4, 4))
                    dve.tensor_reduce(ls[:, 0:1], lp[:, b.par, :], AX.X, ALU.add).then_inc(ln[1], 1)
                    dve.wait_ge(ln[1], b.after(6, 1))
                    dve.reciprocal(ls[:, 1:2], ls[:, 0:1]).then_inc(ln[1], 1)
                    dve.wait_ge(ln[1], b.after(6, 2))
                    dve.wait_ge(pv_done, b.after(8, 8))
                    add_scaled(1, b, 2, ls[:, 1:2])
                    moments(1, b, 4)
                if c == 4:
                    dve.wait_ge(xn_done, over(b, 1, 1, 1))
                    if b.needs(1, 0):
                        dve.wait_ge(xT_done, over(b, 1, 1, 0))
                    dve.tensor_scalar(ba[:, :], xn[:, b.par, :], 0.0, None, ALU.is_gt).then_inc(bin_done, 1)
                if c == 5:
                    dve.wait_ge(xT_done, over(b, 1, 1, 1))
                    if b.needs(1, 0):
                        dve.wait_ge(xw_mm, b.after(1, 0))
                    dve.tensor_copy(baT[:, :, :].rearrange("p c n -> p (c n)"), E0[:, 0:D]).then_inc(binT_done, 1)

            def slot1(b, c):
                if b.exists():
                    add_adj(b, c)
                    if c == CHUNKS - 1:
                        row_max(b)
                t = b.at(-1) if c >= 1 else b.at(-2)
                if t.exists():
                    tc = (c - 1) % CHUNKS
                    chunk_lo(t, tc, hi1, T1[tc % 2], lo1)
                if b.at(-2).exists():
                    end1(b.at(-2), c)

            for off in range(2):
                for c in range(CHUNKS):
                    if off == 0:
                        if c == 0:
                            end0_v(Blk(0, NB - 2))
                            end0_u(Blk(0, NB - 1))
                            moments(0, Blk(0, NB - 1), 1)
                    if off == 1 and c == 7:
                        dve.wait_ge(w23_in, 32)
                        dve.tensor_scalar(w2_sign[:, :, :], w2_stage[:, :, :], 0.0, None, ALU.is_lt).then_inc(w23_ready, 1)
                        dve.wait_ge(w23_ready, 1)
                        dve.scalar_tensor_tensor(w2_sign[:, :, :], w2_stage[:, :, :], 0.0,
                                                 f32(w2_sign[:, :, :]), ALU.is_gt,
                                                 ALU.subtract).then_inc(w23_ready, 1)
                        dve.wait_ge(w3_hi, 1)
                        dve.tensor_tensor(w3_hl[:, 1, :, :], w3_stage[:, :, :], f32(w3_hl[:, 0, :, :]),
                                          ALU.subtract).then_inc(w23_ready, 1)
                    slot1(Blk(0, off), c)
                    if off == 0:
                        if c == 2:
                            split_xT(Blk(0, NB - 1), NB)
                        if c == 3:
                            end0_kq(Pair(0, PAIRS - 1), 0)
                            end0_v(Blk(0, NB - 1))
                        if c == 6:
                            end0_kq(Pair(0, PAIRS - 1), 1)
            with dve.Fori(1, PAIRS) as n:
                for off in range(2):
                    for c in range(CHUNKS):
                        slot1(Blk(n, off), c)
            def piece_lo(layer, b, p):
                dve.wait_ge(hi2, over(b, layer - 2, 4, p + 1))
                dve.tensor_tensor(piece_hl[:, p, 1, :], a_buf[b.par][:, p * PW:(p + 1) * PW],
                                  f32(piece_hl[:, p, 0, :]), ALU.subtract).then_inc(lo2, 1)

            for c in range(CHUNKS):
                slot1(Blk(0, NB), c)
                if c % 2:
                    piece_lo(2, Blk(0, 0), c // 2)
            for c in range(1):
                slot1(Blk(0, NB + 1), c)

            def end2(b, stage):
                if stage == 0:
                    start_end(2, b)
                    dve.wait_ge(mm2, b.after(4, 4))
                    dve.scalar_tensor_tensor(u[:, :], O[b.par][:, 0:D], 0.0, xres[:, b.par, :], ALU.max,
                                             ALU.add).then_inc(ln[2], 1)
                    moments(2, b, 1)
                if stage == 1:
                    split_xT(b, over(b, 1, 1, 1))
                if stage == 2:
                    dve.wait_ge(y_hi, b.after(1, 1))
                    dve.scalar_tensor_tensor(yhl[:, b.rows(), D:2 * D], E0[:, 0:D],
                                             dinv[:, bass.ds(b.rows(), 1)], f32(yhl[:, b.rows(), 0:D]),
                                             ALU.mult, ALU.subtract).then_inc(y_lo, 1)

            def end3(b):
                s, o = ln[3], O[b.par]
                start_end(3, b)
                dve.wait_ge(mm2, over(b, 1, 4, 4))
                dve.tensor_tensor(u[:, :], o[:, 0:D], f32(yhl[:, b.rows(), 0:D]), ALU.add).then_inc(s, 1)
                dve.wait_ge(s, b.after(7, 1))
                dve.tensor_tensor(u[:, :], o[:, D:2 * D], u[:, :], ALU.add).then_inc(s, 1)
                dve.wait_ge(s, b.after(7, 2))
                dve.tensor_tensor(u[:, :], u[:, :], f32(yhl[:, b.rows(), D:2 * D]), ALU.add).then_inc(s, 1)
                dve.wait_ge(s, b.after(7, 3))
                dve.tensor_scalar(u[:, :], u[:, :], 0.0, dinv[:, bass.ds(b.rows(), 1)], ALU.max,
                                  ALU.mult).then_inc(s, 1)
                dve.wait_ge(s, b.after(7, 4))
                dve.tensor_tensor(u[:, :], u[:, :], xres[:, b.par, :], ALU.add).then_inc(s, 1)
                moments(3, b, 5)

            def body2(layer, b, has_next=True):
                prev_layer, prev = ahead(layer, b, -1)
                for p in range(PIECES):
                    if p == 0 and prev_layer == 1:
                        end1(prev, 5)
                    if p == 3:
                        if layer == 2:
                            end2(b, 0)
                        else:
                            end3(b)
                    if has_next:
                        piece_lo(layer, b.at(1), p)
                    if p == 1 and prev_layer == 2:
                        end2(prev, 1)
                    if p == (3 if layer == 2 else 2) and prev_layer == 2:
                        end2(prev, 2)

            end1(Blk(0, NB - 1), 2)
            end1(Blk(0, NB - 1), 4)
            for layer in (2, 3):
                for off in range(2):
                    body2(layer, Blk(0, off))
                with dve.Fori(1, PAIRS - 1) as n:
                    for off in range(2):
                        body2(layer, Blk(n, off))
                for off in range(2):
                    body2(layer, Blk(PAIRS - 1, off), has_next=(layer, off) != (3, 1))

        @block.gpsimd
        def _(pool):
            pool.memset(f32(ones[:, :]), 1.0).then_inc(memsets, 1)
            for i, value in enumerate(CONSTANTS[:-1]):
                pool.memset(const[:, i:i + 1], value)
            pool.memset(const[:, len(CONSTANTS) - 1:], CONSTANTS[-1]).then_inc(memsets, 1)
            pool.memset(b_stage[:, :], 0.0).then_inc(memsets, 1)
            pool.wait_ge(memsets, 3)

            def row_statistics(b):
                s, q = st[:, b.par, :], part[:, b.par, :, :]

                pool.wait_ge(counted, b.after(4, 4))
                pool.wait_ge(summed, b.after(4, 4))
                if b.needs(1, -1):
                    pool.wait_ge(rdeg, b.at(-2).after(1, 1))
                pool.tensor_tensor(st[:, b.par, 12:16].rearrange("p (a c) -> p a c", a=2), q[:, :, 0:2],
                                   q[:, :, 2:4], ALU.add).then_inc(stats, 1)
                pool.wait_ge(stats, b.after(10, 1))
                pool.tensor_tensor(s[:, 0:2], s[:, 12:16:2], s[:, 13:16:2], ALU.add).then_inc(stats, 1)
                pool.wait_ge(stats, b.after(10, 2))
                pool.tensor_tensor(s[:, 2:3], s[:, 0:1], const[:, C_HALF:C_HALF + 1],
                                   ALU.pow).then_inc(stats, 1)
                pool.tensor_tensor(s[:, 3:4], s[:, 1:2], const[:, C_ONE:C_ONE + 1],
                                   ALU.add).then_inc(stats, 1)
                pool.wait_ge(head_scale, b.after(2, 2))
                pool.tensor_tensor(s[:, 5:6], s[:, 3:4], rr[:, b.par, 3:4], ALU.add).then_inc(stats, 1)
                pool.wait_ge(stats, b.after(10, 5))
                pool.tensor_tensor(s[:, 6:7], s[:, 5:6], const[:, C_MHALF:C_MHALF + 1],
                                   ALU.pow).then_inc(stats, 1)
                pool.tensor_tensor(s[:, 7:8], const[:, C_ONE:C_ONE + 1], rr[:, b.par, 3:4],
                                   ALU.subtract).then_inc(stats, 1)
                pool.wait_ge(stats, b.after(10, 7))
                pool.tensor_tensor(dinv[:, bass.ds(b.rows(), 1)], s[:, 6:7], s[:, 7:8],
                                   ALU.mult).then_inc(stats, 1)
                pool.tensor_tensor(s[:, 8:9], rr[:, b.par, 0:1], s[:, 1:2], ALU.mult).then_inc(stats, 1)
                pool.wait_ge(stats, b.after(10, 9))
                pool.tensor_tensor(s[:, 9:10], s[:, 8:9], s[:, 0:1], ALU.add).then_inc(stats, 1)

            def add_residual(b):
                pool.wait_ge(o_scaled, b.after(1, 1))
                pool.wait_ge(xres_in[b.par], b.landed())
                if b.needs(1, 0):
                    pool.wait_ge(xn_done, b.after(1, 0))
                pool.tensor_tensor(u[:, :], xn[:, b.par, :], xres[:, b.par, :], ALU.add).then_inc(o_plus_x, 1)

            def norm_statistics(layer, b):
                steps = LN_STEPS[layer]
                pool.wait_ge(ln[layer], b.after(steps, steps))
                if layer > 0 or b.needs(1, 0):
                    pool.wait_ge(xn_done, over(b, layer, 1, 0))
                pool.tensor_tensor(norm[:, 0:1], mv[:, 1:2], const[:, C_LN_EPS:C_LN_EPS + 1], ALU.add).then_inc(normed, 1)
                pool.wait_ge(normed, over(b, layer, 4, 1))
                pool.tensor_tensor(norm[:, 1:2], norm[:, 0:1], const[:, C_MHALF:C_MHALF + 1], ALU.pow).then_inc(normed, 1)
                pool.wait_ge(normed, over(b, layer, 4, 2))
                pool.tensor_tensor(norm[:, 3:4], mv[:, 0:1], norm[:, 1:2], ALU.mult).then_inc(normed, 1)
                pool.wait_ge(normed, over(b, layer, 4, 3))
                pool.tensor_tensor(norm[:, 2:3], const[:, C_ZERO:C_ZERO + 1], norm[:, 3:4], ALU.subtract).then_inc(normed, 1)

            def split_x(c):
                pool.wait_ge(x_hi, c + 1)
                tiles = slice(c * TPC, (c + 1) * TPC)
                pool.tensor_tensor(xhl[:, tiles, D:2 * D], x_stage[:, tiles, :], f32(xhl[:, tiles, 0:D]),
                                   ALU.subtract).then_inc(x_lo, 1)

            row_statistics(Blk(0, 0))
            for c in range(CHUNKS - 2):
                split_x(c)
            row_statistics(Blk(0, 1))
            for c in range(CHUNKS - 2, CHUNKS):
                split_x(c)
            pool.wait_ge(w_hi, 4)
            pool.tensor_tensor(w_hl[:, 1, :, :], w_stage[:, :, :], f32(w_hl[:, 0, :, :]),
                               ALU.subtract).then_inc(w_lo, 1)
            pool.wait_ge(w_lo, 1)
            pool.tensor_tensor(b_r[32:33, :], b_stage[32:33, :], f32(b_r[32:33, :]),
                               ALU.subtract).then_inc(bias_ready, 1)
            pool.wait_ge(bias_ready, 1)
            with pool.Fori(1, PAIRS) as n:
                for off in range(2):
                    add_residual(Blk(n, off - 2))
                    norm_statistics(0, Blk(n, off - 2))
                    row_statistics(Blk(n, off))
            for off in range(2):
                add_residual(Blk(PAIRS, off - 2))
                norm_statistics(0, Blk(PAIRS, off - 2))
            for layer in range(1, 4):
                with pool.Fori(0, PAIRS) as n:
                    for off in range(2):
                        norm_statistics(layer, Blk(n, off))


def kernel(x, adj, L1_gnn_Wq, L1_gnn_bq, L1_gnn_Wk, L1_gnn_bk, L1_gnn_Wv, L1_gnn_bv, L2_gnn_weight,
           L3_gnn_weight):
    import numpy as np
    import concourse.bacc as bacc
    from concourse.bass_utils import run_bass_kernel_spmd

    x, adj = np.ascontiguousarray(x), np.ascontiguousarray(adj)
    arrays = {
        "x_in": x,
        "adj": adj,
        "adjT": np.ascontiguousarray(adj.reshape(NB, P, NB, P).transpose(0, 3, 2, 1)).reshape(NB, P, N),
        "wkqv": np.ascontiguousarray(np.concatenate(
            [np.asarray(w).T for w in (L1_gnn_Wk, L1_gnn_Wq, L1_gnn_Wv)], axis=1)),
        "bias": np.concatenate([np.asarray(b) for b in (L1_gnn_bk, L1_gnn_bq, L1_gnn_bv)]).reshape(1, 3 * D),
        "w2t": np.ascontiguousarray(np.asarray(L2_gnn_weight).T),
        "w3": np.ascontiguousarray(L3_gnn_weight),
        "ident_in": np.eye(P, dtype=np.float32),
    }
    nc = bacc.Bacc("TRN2", target_bir_lowering=False, num_devices=1, dynamic_dma_scratch_size=1024)
    args = {n: nc.dram_tensor(n, a.shape, mybir.dt.from_np(a.dtype), kind="ExternalInput").ap()
            for n, a in arrays.items()}
    args["out"] = nc.dram_tensor("out", (N, D), F32, kind="ExternalOutput").ap()
    build(nc, **args)
    r = run_bass_kernel_spmd(nc, [arrays], core_ids=[0])
    return r.results[0]["out"]
```

```python
import concourse.bass as bass
from concourse import mybir
from contextlib import ExitStack

P = 128
N = 4096
D = 256
NB = N // P
CHUNKS = 8
CW = N // CHUNKS
TPC = CW // P
PIECES = 4
PW = N // PIECES
TPP = PW // P
DC = D // P
LN_EPS = 1e-5
HEAD_EPS = 1e-12
PAIRS = NB // 2
CONSTANTS = (0.5, -0.5, LN_EPS, 1.0, 0.0)
C_HALF, C_MHALF, C_LN_EPS, C_ONE, C_ZERO = range(len(CONSTANTS))

F32 = mybir.dt.float32
F32R = mybir.dt.float32r
BF16 = mybir.dt.bfloat16
U8 = mybir.dt.uint8
ALU = mybir.AluOpType
ACT = mybir.ActivationFunctionType
AX = mybir.AxisListType


class Blk:

    def __init__(self, n, off):
        self.n, self.off = n, off
        self.par = off % 2

    def at(self, shift):
        return Blk(self.n, self.off + shift)

    @property
    def number(self):
        return 2 * self.n + self.off

    def exists(self):
        return not isinstance(self.n, int) or 0 <= self.number < NB

    def after(self, per_block, k):
        return 2 * per_block * self.n + per_block * self.off + k

    def needs(self, per_block, k):
        return not isinstance(self.n, int) or self.after(per_block, k) > 0

    def landed(self, layer=0):
        return 16 * self.n + 16 * (self.off // 2 + 1 + PAIRS * layer)

    def rows(self):
        return self.number


class Pair:

    def __init__(self, n, off):
        self.n, self.off = n, off

    @property
    def number(self):
        return self.n + self.off

    def after(self, per_pair, k):
        return per_pair * self.n + per_pair * self.off + k

    def needs(self, per_pair, k):
        return not isinstance(self.n, int) or self.after(per_pair, k) > 0

    def exists(self):
        return not isinstance(self.n, int) or self.number >= 0


def build(nc, x_in, adj, adjT, wkqv, bias_kq_in, bias_v, w2t, w3, ident_in, out):
    ctx = ExitStack()
    with ctx:
        def sb(name, shape, dt):
            return ctx.enter_context(nc.sbuf_tensor(name, shape, dt))

        def overlay(*groups):
            made = []
            for i, group in enumerate(groups):
                stack = ctx if i == len(groups) - 1 else ExitStack()
                made += [stack.enter_context(nc.sbuf_tensor(*t)) for t in group]
                if stack is not ctx:
                    stack.close()
            return made

        def sem(name):
            return ctx.enter_context(nc.semaphore(name))

        ident = sb("ident", [P, P], F32)
        ones = sb("ones", [P, P], F32R)
        const = sb("const", [P, len(CONSTANTS)], F32)
        dinv = sb("dinv", [P, NB], F32)
        xhl, vhl, yhl = overlay([("xhl", [P, NB, 2 * D], F32R)], [("vhl", [P, NB, 2 * D], F32R)],
                                [("yhl", [P, NB, 2 * D], F32R)])
        x_stage, w_stage, b_stage, xw, piece_hl, kT = overlay(
            [("x_stage", [P, NB, D], F32), ("w_stage", [P, DC, 3 * D], F32), ("b_stage", [P, D], F32)],
            [("xw", [P, NB, D], F32R), ("piece_hl", [P, PIECES, 2, PW], F32R)],
            [("kT", [P, 2, DC, N], F32R)])
        a_buf = [sb(f"a_buf{i}", [P, N], F32) for i in range(2)]
        chunk_hl = sb("chunk_hl", [P, 4, 2, CW], F32R)
        xres = sb("xres", [P, 2, D], F32)
        u = sb("u", [P, D], F32)
        xn = sb("xn", [P, 2, D], F32)
        xT = sb("xT", [P, 2, DC, 2, P], F32R)
        settle = sb("settle", [1, CHUNKS + 1], F32)
        bn6 = sb("bn6", [P, 6], F32)
        mv = sb("mv", [P, 2], F32)
        norm = sb("norm", [P, 4], F32)
        part = sb("part", [P, 2, 2, PIECES], F32)
        st = sb("st", [P, 2, 16], F32)
        rr = sb("rr", [P, 2, 4], F32)
        qt = sb("qt", [P, 2, 2, D], F32R)
        mxp = sb("mxp", [P, 2, CHUNKS], F32)
        mx = sb("mx", [P, 2, 2], F32)
        lp = sb("lp", [P, 2, PIECES], F32)
        ls = sb("ls", [P, 2], F32)
        (w2_stage, w3_stage, w3_hl, w2_sign, ba, baT, xw_out,
         w_hl, b_r, bias_kq, mask, junk_act, kq_hl, v_hl) = overlay(
            [("w2_stage", [P, DC, D], F32), ("w3_stage", [P, DC, D], F32), ("w3_hl", [P, 2, DC, D], F32R),
             ("w2_sign", [P, DC, D], F32R), ("ba", [P, D], F32), ("baT", [P, DC, P], F32R),
             ("xw_out", [P, D], F32R)],
            [("w_hl", [P, 2, DC, 3 * D], F32R), ("b_r", [P, D], F32R), ("bias_kq", [P, 2 * DC], F32),
             ("mask", [P, N], U8), ("junk_act", [P, PW], BF16), ("kq_hl", [P, 2, 2, DC, 2 * P], F32R),
             ("v_hl", [P, 2, 2 * D], F32R)])

        banks = [ctx.enter_context(nc.psum_tensor(f"bank{i}", [P, 512], F32)) for i in range(8)]
        T0 = banks[0:4]
        S1, T1 = banks[0:2], banks[2:4]
        O = banks[4:6]
        E0, E1 = banks[6], banks[7]

        def dram(name, shape, dt):
            return nc.dram_tensor(name, shape, dt).ap()

        def f32(ap):
            return ap.bitcast(F32)

        x_mid = [dram(f"x_mid{i}", [N, D], F32) for i in range(3)]
        x_of = [x_in] + x_mid + [out]
        q_scr = dram("q_scr", [PAIRS, P, 2 * DC, 2, P], F32)
        v_scr = dram("v_scr", [NB, P, 2 * D], F32)
        xw_scr = dram("xw_scr", [NB, P, D], F32)

        def x_rows(layer, b):
            return x_of[layer].rearrange("(b p) d -> b p d", p=P)[b.rows()]

        const_in = sem("const_in")
        bias_in = sem("bias_in")
        x_stage_in = [sem(f"x_stage_in{c}") for c in range(CHUNKS)]
        a_in = [[sem(f"a_in{par}_{p}") for p in range(PIECES)] for par in range(2)]
        xres_in = [sem(f"xres_in{par}") for par in range(2)]
        x_out = [sem(f"x_out{par}") for par in range(2)]
        k_placed, q_stored = sem("k_placed"), sem("q_stored")
        v_stored = [sem(f"v_stored{par}") for par in range(2)]
        q_in = [sem(f"q_in{par}") for par in range(2)]
        v_in = [sem(f"v_in{c}") for c in range(CHUNKS)]
        w23_in = sem("w23_in")
        xw_stored = sem("xw_stored")
        xw_in = sem("xw_in")
        memsets = sem("memsets")
        x_hi, x_lo = sem("x_hi"), sem("x_lo")
        w_hi, w_lo = sem("w_hi"), sem("w_lo")
        bias_ready = sem("bias_ready")
        w23_ready, w3_hi = sem("w23_ready"), sem("w3_hi")
        counted = sem("counted")
        summed = sem("summed")
        stats = sem("stats")
        head_scale = sem("head_scale")
        rdeg = sem("rdeg")
        inc_done = sem("inc_done")
        t0_done = sem("t0_done")
        hi0, lo0 = sem("hi0"), sem("lo0")
        mm0 = sem("mm0")
        v_mm, v_hi, v_raw, v_lo = sem("v_mm"), sem("v_hi"), sem("v_raw"), sem("v_lo")
        o_scaled = sem("o_scaled")
        o_plus_x = sem("o_plus_x")
        kq_mm, kq_hi, kq_raw, kq_lo = sem("kq_mm"), sem("kq_hi"), sem("kq_raw"), sem("kq_lo")
        qk_done = sem("qk_done")
        scored = sem("scored")
        maxed = sem("maxed")
        exped = sem("exped")
        t1_done = sem("t1_done")
        hi1, lo1 = sem("hi1"), sem("lo1")
        pv_done = sem("pv_done")
        bin_done, binT_done = sem("bin_done"), sem("binT_done")
        xw_mm, xw_copied = sem("xw_mm"), sem("xw_copied")
        hi2, lo2, mm2 = sem("hi2"), sem("lo2"), sem("mm2")
        y_mm, y_hi, y_lo = sem("y_mm"), sem("y_hi"), sem("y_lo")
        LN_STEPS = [3, 6, 3, 7]
        ln = [sem(f"ln{i}") for i in range(4)]
        normed = sem("normed")
        xn_done = sem("xn_done")
        xT_done = sem("xT_done")
        xT_hi, xT_lo = sem("xT_hi"), sem("xT_lo")

        block = ctx.enter_context(nc.Block())

        def ahead(layer, b, k):
            if not isinstance(b.n, int):
                return layer, b.at(k)
            return layer + (b.number + k) // NB, Blk(0, (b.number + k) % NB)

        def over(b, layer, per_block, k):
            return b.after(per_block, k) + per_block * NB * layer

        @block.sync
        def _(sp):
            def load_a(layer, b, p):
                sp.dma_start(a_buf[b.par][:, p * PW:(p + 1) * PW],
                             (adj.rearrange("(b p) n -> b p n", p=P) if layer < 2 else adjT)[b.rows()]
                             [:, p * PW:(p + 1) * PW]).then_inc(a_in[b.par][p], 16)

            def load_xres(layer, b):
                if layer > 0:
                    sp.wait_ge(x_out[b.par], 16 * PAIRS * layer)
                sp.dma_start(xres[:, b.par, :], x_rows(layer, b)).then_inc(xres_in[b.par], 16)

            def store_x(layer, b):
                sp.wait_ge(xn_done, over(b, layer, 1, 1))
                sp.dma_start(x_rows(layer + 1, b), xn[:, b.par, :]).then_inc(x_out[b.par], 16)

            def read0(b, p):
                sp.wait_ge(t0_done, b.after(8, 2 * p + 2))

            def store_k(m):
                sp.wait_ge(kq_hi, m.after(4, 2))
                sp.wait_ge(kq_lo, m.after(2, 1))
                for h in range(2):
                    sp.dma_start(f32(kT[:, h, :, bass.ds(m.number * 2 * P, 2 * P)]),
                                 f32(kq_hl[:, 0, h, :, :])).then_inc(k_placed, 16)

            def store_q(m):
                sp.wait_ge(kq_hi, m.after(4, 4))
                sp.wait_ge(kq_lo, m.after(2, 2))
                sp.dma_start(q_scr[m.number].rearrange("p c b i -> p (c b i)"),
                             f32(kq_hl[:, 1, :, :, :]).rearrange("p h c n -> p (h c n)")).then_inc(q_stored, 16)

            def store_v(b):
                sp.wait_ge(v_lo, b.after(1, 1))
                sp.dma_start(v_scr[b.rows()], f32(v_hl[:, b.par, :])).then_inc(v_stored[b.par], 16)

            def body0(b, layer, nxt):
                pair = Pair(b.n, b.off // 2 - 1)
                if b.needs(1, -1):
                    sp.wait_ge(ln[0], b.at(-2).after(3, 1))
                load_xres(0, b)
                read0(b, 0)
                load_a(layer, nxt, 0)
                read0(b, 1)
                load_a(layer, nxt, 1)
                if b.at(-3).exists():
                    store_v(b.at(-3))
                read0(b, 2)
                load_a(layer, nxt, 2)
                read0(b, 3)
                load_a(layer, nxt, 3)
                if b.at(-1).exists():
                    store_x(0, b.at(-1))
                if b.par and pair.exists():
                    store_k(pair)
                    store_q(pair)

            first, second = Blk(0, 0), Blk(0, 1)
            sp.dma_start(a_buf[0][:, 0:PW], adj[0:P, 0:PW]).then_inc(a_in[0][0], 16)

            def load_x_stage(c):
                tiles = slice(c * TPC, (c + 1) * TPC)
                sp.dma_start(x_stage[:, tiles, :], x_in.rearrange("(t p) d -> p t d", p=P)[:, tiles, :]
                             ).then_inc(x_stage_in[c], 16)

            load_x_stage(0)
            sp.dma_start(ident[:, :], ident_in).then_inc(const_in, 16)
            for p in range(1, PIECES):
                load_a(0, first, p)
            load_x_stage(1)
            load_x_stage(2)
            load_a(0, second, 0)
            load_x_stage(3)
            load_x_stage(4)
            load_a(0, second, 1)
            load_a(0, second, 2)
            load_x_stage(5)
            load_x_stage(6)
            load_a(0, second, 3)
            load_x_stage(7)
            sp.dma_start(w_stage[:, :, :], wkqv.rearrange("(c p) n -> p c n", p=P)).then_inc(const_in, 16)
            sp.wait_ge(memsets, 3)
            sp.dma_start(b_stage[0:1, :], bias_v).then_inc(bias_in, 16)
            sp.dma_start(b_stage[32:33, :], bias_v).then_inc(bias_in, 16)
            sp.dma_start(bias_kq[:, :], bias_kq_in).then_inc(bias_in, 16)

            for off in range(4):
                body0(Blk(0, off), 0, Blk(0, off + 2))
            with sp.Fori(2, PAIRS - 1) as n:
                for off in range(2):
                    body0(Blk(n, off), 0, Blk(n, off + 2))
            def load_q(b):
                sp.dma_start(f32(qt[:, b.par, :, :]).rearrange("p h (c i) -> p (h c) i", c=DC),
                             q_scr[b.n + b.off // 2][:, :, b.par, :]).then_inc(q_in[b.par], 16)

            sp.wait_ge(q_stored, 16 * (PAIRS - 2))
            for off in range(2):
                load_q(Blk(0, off))
            for off in range(2):
                body0(Blk(PAIRS - 1, off), 1, Blk(0, off))

            def store_xw(b):
                sp.wait_ge(xw_copied, b.after(1, 1))
                sp.dma_start(xw_scr[b.rows()], f32(xw_out[:, :])).then_inc(xw_stored, 16)

            def body1(b, nxt, layer):
                if b.at(-2).exists():
                    sp.wait_ge(t1_done, b.at(-2).after(8, 8))
                    load_a(1, b, 3)
                if b.needs(1, 0):
                    sp.wait_ge(qk_done, b.at(-1).after(8, 8))
                if not isinstance(b.n, int) or b.number > 0:
                    sp.wait_ge(q_stored, 16 * PAIRS)
                    load_q(nxt)
                for p in range(3):
                    if b.at(-1).exists():
                        sp.wait_ge(t1_done, b.at(-1).after(8, 2 * p + 2))
                        load_a(layer, nxt, p)
                    if p == 0:
                        if b.at(-2).exists():
                            store_x(1, b.at(-2))
                            sp.wait_ge(ln[1], b.at(-2).after(6, 4))
                        else:
                            sp.wait_ge(ln[0], 3 * (NB - 2 + b.number) + 1)
                        load_xres(1, b)
                if b.at(-2).exists():
                    store_xw(b.at(-2))

            def load_v(c):
                sp.dma_start(f32(vhl[:, c * TPC:(c + 1) * TPC, :]),
                             v_scr.rearrange("b p n -> p b n")[:, c * TPC:(c + 1) * TPC, :]).then_inc(v_in[c], 16)

            store_v(Blk(0, NB - 3))
            sp.wait_ge(mm0, 8 * NB)
            for par in range(2):
                sp.wait_ge(v_stored[par], 16 * (PAIRS - 1))
            for c in range(2):
                load_v(c)
            store_v(Blk(0, NB - 2))
            store_x(0, Blk(0, NB - 1))
            store_k(Pair(0, PAIRS - 1))
            store_v(Blk(0, NB - 1))
            for c in range(2, 5):
                load_v(c)
            body1(Blk(0, 0), Blk(0, 1), 1)
            store_q(Pair(0, PAIRS - 1))
            load_v(5)
            load_v(6)
            for par in range(2):
                sp.wait_ge(v_stored[par], 16 * PAIRS)
            load_v(7)
            sp.wait_ge(k_placed, 32 * PAIRS)
            sp.wait_ge(q_stored, 16 * PAIRS)
            sp.wait_ge(v_mm, NB)
            sp.dma_start(w2_stage[:, :, :], w2t.rearrange("(c p) n -> p c n", p=P)).then_inc(w23_in, 16)
            sp.dma_start(w3_stage[:, :, :], w3.rearrange("(c p) n -> p c n", p=P)).then_inc(w23_in, 16)
            body1(Blk(0, 1), Blk(0, 2), 1)
            with sp.Fori(1, PAIRS - 1) as n:
                for off in range(2):
                    body1(Blk(n, off), Blk(n, off + 1), 1)
            body1(Blk(PAIRS - 1, 0), Blk(PAIRS - 1, 1), 1)
            last = Blk(0, NB - 1)
            sp.wait_ge(t1_done, last.at(-2).after(8, 8))
            load_a(1, last, 3)
            for p in range(PIECES):
                sp.wait_ge(t1_done, last.at(-1).after(8, 2 * p + 2))
                load_a(2, Blk(0, 0), p)
                if p == 0:
                    store_x(1, last.at(-2))
                    sp.wait_ge(ln[1], last.at(-2).after(6, 4))
                    load_xres(1, last)
                if p == 2:
                    store_xw(last.at(-2))
            sp.wait_ge(qk_done, 8 * NB)
            sp.wait_ge(xw_stored, 16 * (NB - 2))
            sp.dma_start(f32(xw[:, 0:NB - 2, :]), xw_scr.rearrange("b p n -> p b n")[:, 0:NB - 2, :]).then_inc(xw_in, 16)
            store_x(1, last.at(-1))
            sp.wait_ge(ln[1], last.at(-1).after(6, 4))
            load_xres(2, Blk(0, 0))
            for p in range(PIECES):
                sp.wait_ge(t1_done, last.after(8, 2 * p + 2))
                load_a(2, Blk(0, 1), p)
            for p in range(PIECES):
                sp.wait_ge(lo2, p + 1)
                load_a(2, Blk(0, 2), p)

            def body2(layer, b):
                for p in range(PIECES):
                    to_layer, to = ahead(layer, b, 3)
                    if to_layer < 4:
                        sp.wait_ge(lo2, over(b.at(1), layer - 2, 4, p + 1))
                        load_a(to_layer, to, p)
                    if p == 0:
                        prev_layer, prev = ahead(layer, b, -1)
                        store_x(prev_layer, prev)
                        to_layer, to = ahead(layer, b, 1)
                        if to_layer < 4:
                            steps = LN_STEPS[prev_layer]
                            sp.wait_ge(ln[prev_layer], prev.after(steps, steps - 2))
                            load_xres(to_layer, to)

            for layer in (2, 3):
                for off in range(2):
                    body2(layer, Blk(0, off))
                with sp.Fori(1, PAIRS - 2) as n:
                    for off in range(2):
                        body2(layer, Blk(n, off))
                for off in range(4):
                    body2(layer, Blk(PAIRS - 2, off))
            store_x(3, last)
            for par in range(2):
                sp.wait_ge(x_out[par], 16 * PAIRS * 4)

        @block.tensor
        def _(pe):
            def transpose0(b, c):
                pe.wait_ge(inc_done, b.after(8, c + 1))
                if b.needs(8, c - 3):
                    pe.wait_ge(lo0, b.after(8, c - 3))
                for t in range(TPC):
                    cols = slice(t * P, (t + 1) * P)
                    mm = pe.transpose(T0[c % 4][:, cols], a_buf[b.par][:, c * CW + t * P:c * CW + (t + 1) * P], ident[:, :])
                mm.then_inc(t0_done, 1)

            def by_hi_lo(b, c, values, done):
                o = O[b.par]
                for t in range(TPC):
                    j = c * TPC + t
                    hi = chunk_hl[:, c % 4, 0, t * P:(t + 1) * P]
                    lo = chunk_hl[:, c % 4, 1, t * P:(t + 1) * P]
                    if j < NB - 1:
                        pe.matmul(o[:, :], hi, values[:, j, :], start=(j == 0), stop=False)
                        mm = pe.matmul(o[:, D:2 * D], lo, values[:, j, 0:D], start=False, stop=False)
                    else:
                        pe.matmul(o[:, D:2 * D], lo, values[:, j, 0:D], start=False, stop=False)
                        mm = pe.matmul(o[:, :], hi, values[:, j, :], start=False, stop=True)
                mm.then_inc(done, 1)

            def products0(b, c):
                pe.wait_ge(lo0, b.after(8, c + 1))
                if isinstance(b.n, int) and b.number == 0:
                    pe.wait_ge(x_lo, c + 1)
                if c == 0 and b.needs(1, -1):
                    pe.wait_ge(ln[0], b.at(-2).after(3, 1))
                by_hi_lo(b, c, xhl, mm0)

            def block_transpose(layer, b, src, ready, value):
                pe.wait_ge(ready, value)
                for dc in range(DC):
                    mm = pe.transpose(E0[:, dc * P:(dc + 1) * P], src[:, dc * P:(dc + 1) * P], ident[:, :])
                mm.then_inc(xT_done, 1)

            def end0_transpose(b):
                if b.needs(1, 0):
                    pe.wait_ge(v_raw if b.par else xT_lo, b.after(1, 0))
                block_transpose(0, b, xn[:, b.par, :], xn_done, b.after(1, 1))

            def end0_v(b):
                latest = b.at(b.par) if b.at(b.par).exists() else b
                pe.wait_ge(xT_hi, latest.after(1, 1))
                pe.wait_ge(xT_lo, latest.after(1, 1))
                if not b.par and b.needs(1, 0):
                    pe.wait_ge(v_raw, b.after(1, 0))
                if isinstance(b.n, int) and b.number == 0:
                    pe.wait_ge(w_lo, 1)
                    pe.wait_ge(bias_ready, 1)
                v = slice(2 * D, 3 * D)
                x_hi, x_lo = xT[:, 0, :, b.par, :], xT[:, 1, :, b.par, :]
                pe.matmul(E0[:, 0:D], ones[:, :], b_r[:, :], start=True, stop=False)
                for dc in range(DC):
                    pe.matmul(E0[:, 0:D], x_lo[:, dc, :], w_hl[:, 0, dc, v], start=False, stop=False)
                    pe.matmul(E0[:, 0:D], x_hi[:, dc, :], w_hl[:, 1, dc, v], start=False, stop=False)
                    mm = pe.matmul(E0[:, 0:D], x_hi[:, dc, :], w_hl[:, 0, dc, v],
                                   start=False, stop=(dc == DC - 1))
                mm.then_inc(v_mm, 1)

            def end0_kq(m, which):
                for g in range(DC):
                    end0_kq_half(m, which, g)

            def end0_kq_half(m, which, g):
                if g == 0:
                    if m.needs(2, which):
                        pe.wait_ge(kq_raw, m.after(4, 2 * which))
                    if which == 0:
                        pe.wait_ge(xT_hi, m.after(2, 2))
                        pe.wait_ge(xT_lo, m.after(2, 2))
                out_cols = slice(g * 2 * P, (g + 1) * 2 * P)
                cols = slice((which * DC + g) * P, (which * DC + g + 1) * P)
                for dc in range(DC):
                    x_hi = xT[:, 0, dc, :, :].rearrange("p b i -> p (b i)")
                    x_lo = xT[:, 1, dc, :, :].rearrange("p b i -> p (b i)")
                    pe.matmul(E1[:, out_cols], w_hl[:, 1, dc, cols], x_hi, start=(dc == 0), stop=False)
                    pe.matmul(E1[:, out_cols], w_hl[:, 0, dc, cols], x_lo, start=False, stop=False)
                    mm = pe.matmul(E1[:, out_cols], w_hl[:, 0, dc, cols], x_hi,
                                   start=False, stop=(dc == DC - 1))
                if g == DC - 1:
                    mm.then_inc(kq_mm, 1)

            def slot0(b, c):
                if b.exists():
                    transpose0(b, c)
                prev = b if c >= 3 else b.at(-1)
                if prev.exists():
                    products0(prev, (c - 3) % CHUNKS)
                if b.at(-2).exists() and c == 0:
                    end0_transpose(b.at(-2))
                if not b.par and b.at(-3).exists() and c == 1:
                    end0_v(b.at(-3))
                if not b.par and b.at(-2).exists() and c == 4:
                    end0_v(b.at(-2))
                if b.par and Pair(b.n, b.off // 2 - 1).exists() and c in (2, 3, 5, 6):
                    end0_kq_half(Pair(b.n, b.off // 2 - 1), c // 5, (c - 2) % 3)

            pe.wait_ge(const_in, 16)
            pe.wait_ge(memsets, 1)
            for off in range(4):
                for c in range(CHUNKS):
                    slot0(Blk(0, off), c)
            with pe.Fori(2, PAIRS) as n:
                for off in range(2):
                    for c in range(CHUNKS):
                        slot0(Blk(n, off), c)

            def scores(b, c):
                s = S1[c % 2]
                if c == 0:
                    pe.wait_ge(q_in[b.par], b.landed())
                if isinstance(b.n, int) and b.number == 0:
                    pe.wait_ge(k_placed, 32 * (PAIRS if c == CHUNKS - 1 else PAIRS - 1))
                    if c == 0:
                        pe.wait_ge(lo0, 8 * NB)
                if b.needs(8, c - 1):
                    pe.wait_ge(scored, b.after(8, c - 1))
                q = qt[:, b.par, :, :]
                cols = slice(c * CW, (c + 1) * CW)
                for dc in range(DC):
                    dd = slice(dc * P, (dc + 1) * P)
                    pe.matmul(s[:, :], q[:, 1, dd], kT[:, 0, dc, cols], start=(dc == 0), stop=False)
                    pe.matmul(s[:, :], q[:, 0, dd], kT[:, 1, dc, cols], start=False, stop=False)
                    mm = pe.matmul(s[:, :], q[:, 0, dd], kT[:, 0, dc, cols], start=False, stop=(dc == DC - 1))
                mm.then_inc(qk_done, 1)

            def transpose1(b, c):
                pe.wait_ge(exped, b.after(4, c // 2 + 1))
                if b.needs(8, c - 1):
                    pe.wait_ge(lo1, b.after(8, c - 1))
                for t in range(TPC):
                    mm = pe.transpose(T1[c % 2][:, t * P:(t + 1) * P],
                                      a_buf[b.par][:, c * CW + t * P:c * CW + (t + 1) * P], ident[:, :])
                mm.then_inc(t1_done, 1)

            def products1(b, c):
                pe.wait_ge(lo1, b.after(8, c + 1))
                if isinstance(b.n, int) and b.number == 0:
                    pe.wait_ge(v_in[c], 16)
                    if c == 0:
                        pe.wait_ge(ln[0], 3 * NB)
                by_hi_lo(b, c, vhl, pv_done)

            def end1_transpose(b):
                if b.needs(1, 0):
                    pe.wait_ge(xw_copied, b.after(1, 0))
                block_transpose(1, b, ba, bin_done, b.after(1, 1))

            def end1_xw(b):
                pe.wait_ge(binT_done, b.after(1, 1))
                if isinstance(b.n, int) and b.number == 0:
                    pe.wait_ge(w23_ready, 2)
                for dc in range(DC):
                    mm = pe.matmul(E0[:, 0:D], baT[:, dc, :], w2_sign[:, dc, :], start=(dc == 0), stop=(dc == 1))
                mm.then_inc(xw_mm, 1)

            def slot1(b, c):
                if b.exists():
                    scores(b, c)
                t = b.at(-1) if c >= 1 else b.at(-2)
                if t.exists():
                    transpose1(t, (c - 1) % CHUNKS)
                m = b.at(-1) if c >= 2 else b.at(-2)
                if m.exists():
                    products1(m, (c - 2) % CHUNKS)
                if b.at(-2).exists():
                    if c == (5 if b.exists() else 6):
                        end1_transpose(b.at(-2))
                    if c == (6 if b.exists() else 7):
                        end1_xw(b.at(-2))

            for off in range(2):
                for c in range(CHUNKS):
                    if off == 0:
                        if c == 0:
                            products0(Blk(0, NB - 1), 5)
                            end0_transpose(Blk(0, NB - 2))
                            products0(Blk(0, NB - 1), 6)
                            end0_v(Blk(0, NB - 3))
                            products0(Blk(0, NB - 1), 7)
                    slot1(Blk(0, off), c)
                    if off == 0:
                        if c == 0:
                            end0_v(Blk(0, NB - 2))
                        if c == 2:
                            end0_transpose(Blk(0, NB - 1))
                        if c == 3:
                            end0_kq(Pair(0, PAIRS - 1), 0)
                            end0_v(Blk(0, NB - 1))
                        if c == 4:
                            end0_kq(Pair(0, PAIRS - 1), 1)
            with pe.Fori(1, PAIRS) as n:
                for off in range(2):
                    for c in range(CHUNKS):
                        slot1(Blk(n, off), c)
            for c in range(CHUNKS):
                slot1(Blk(0, NB), c)
            for c in range(2):
                slot1(Blk(0, NB + 1), c)

            def products2(layer, b, p):
                pe.wait_ge(lo2, over(b, layer - 2, 4, p + 1))
                if layer == 2 and isinstance(b.n, int) and b.number == 0:
                    if p == 0:
                        pe.wait_ge(xw_in, 16)
                    if p == PIECES - 1:
                        pe.wait_ge(xw_copied, NB)
                if layer == 3 and isinstance(b.n, int) and b.number == 0:
                    pe.wait_ge(y_lo, NB if p == PIECES - 1 else NB - 2)
                if p == 0:
                    before = b.at(-2)
                    if b.needs(1, -1):
                        pe.wait_ge(ln[layer], before.after(LN_STEPS[layer], LN_STEPS[layer] - 2))
                    else:
                        pe.wait_ge(ln[layer - 1], LN_STEPS[layer - 1] * (NB + b.number - 1) - 2)
                o = O[b.par]
                for t in range(TPP):
                    j = p * TPP + t
                    hi = piece_hl[:, p, 0, t * P:(t + 1) * P]
                    lo = piece_hl[:, p, 1, t * P:(t + 1) * P]
                    if layer == 2:
                        pe.matmul(o[:, 0:D], hi, xw[:, j, :], start=(j == 0), stop=False)
                        mm = pe.matmul(o[:, 0:D], lo, xw[:, j, :], start=False, stop=(j == NB - 1))
                    elif j < NB - 1:
                        pe.matmul(o[:, :], hi, yhl[:, j, :], start=(j == 0), stop=False)
                        mm = pe.matmul(o[:, D:2 * D], lo, yhl[:, j, 0:D], start=False, stop=False)
                    else:
                        pe.matmul(o[:, D:2 * D], lo, yhl[:, j, 0:D], start=False, stop=False)
                        mm = pe.matmul(o[:, :], hi, yhl[:, j, :], start=False, stop=True)
                mm.then_inc(mm2, 1)

            def end2_transpose(b):
                if b.needs(1, 0):
                    pe.wait_ge(y_lo, b.after(1, 0))
                else:
                    pe.wait_ge(xw_copied, NB)
                block_transpose(2, b, xn[:, b.par, :], xn_done, over(b, 2, 1, 1))

            def end2_y(b):
                pe.wait_ge(xT_hi, over(b, 1, 1, 1))
                pe.wait_ge(xT_lo, over(b, 1, 1, 1))
                x_hi, x_lo = xT[:, 0, :, b.par, :], xT[:, 1, :, b.par, :]
                for dc in range(DC):
                    pe.matmul(E0[:, 0:D], x_lo[:, dc, :], w3_hl[:, 0, dc, :], start=(dc == 0), stop=False)
                    pe.matmul(E0[:, 0:D], x_hi[:, dc, :], w3_hl[:, 1, dc, :], start=False, stop=False)
                    mm = pe.matmul(E0[:, 0:D], x_hi[:, dc, :], w3_hl[:, 0, dc, :],
                                   start=False, stop=(dc == DC - 1))
                mm.then_inc(y_mm, 1)

            def body2(layer, b):
                prev_layer, prev = ahead(layer, b, -1)
                for p in range(PIECES):
                    products2(layer, b, p)
                    if prev_layer == 1:
                        if p in (1, 2):
                            (end1_transpose, end1_xw)[p - 1](prev)
                    elif prev_layer == 2:
                        if p == 1:
                            end2_transpose(prev)
                        if p == (3 if layer == 2 else 2):
                            end2_y(prev)

            for layer in (2, 3):
                for off in range(2):
                    body2(layer, Blk(0, off))
                with pe.Fori(1, PAIRS) as n:
                    for off in range(2):
                        body2(layer, Blk(n, off))

        @block.scalar
        def _(act):
            def row_sum(b, p):
                act.wait_ge(a_in[b.par][p], b.landed())
                if b.needs(1, -1):
                    act.wait_ge(stats, b.at(-2).after(10, 1))
                if b.needs(4, p):
                    act.wait_ge(summed, b.after(4, p))
                act.activation(junk_act[:, :], a_buf[b.par][:, p * PW:(p + 1) * PW], ACT.Copy,
                               accum_out=part[:, b.par, 1, p:p + 1]).then_inc(summed, 1)

            def chunk_hi(b, c, transposed, used, t_bank, out_sem):
                act.wait_ge(transposed, b.after(8, c + 1))
                if b.needs(8, c - 3):
                    act.wait_ge(used, b.after(8, c - 3))
                act.activation(chunk_hl[:, c % 4, 0, :], t_bank[:, :], ACT.Copy).then_inc(out_sem, 1)

            def normalise(layer, b):
                act.wait_ge(normed, over(b, layer, 4, 4))
                if layer > 0:
                    act.wait_ge(x_out[b.par], b.at(-2).landed(layer))
                act.activation(xn[:, b.par, :], u[:, :], ACT.Identity, bias=norm[:, 2:3],
                               scale=norm[:, 1:2]).then_inc(xn_done, 1)

            def split_xT(b, t_value, used, used_value):
                act.wait_ge(xT_done, t_value)
                if used is not None:
                    act.wait_ge(used, used_value)
                act.activation(xT[:, 0, :, b.par, :], E0[:, 0:D].rearrange("p (c i) -> p c i", c=DC),
                               ACT.Copy).then_inc(xT_hi, 1)

            def end0_scale(b):
                act.wait_ge(mm0, b.after(8, 8))
                act.wait_ge(rdeg, b.after(1, 1))
                if b.needs(1, -1):
                    act.wait_ge(x_out[b.par], b.at(-2).landed())
                    act.wait_ge(xT_done, b.at(-2).after(1, 1))
                act.activation(xn[:, b.par, :], O[b.par][:, 0:D], ACT.Copy,
                               scale=rr[:, b.par, 1:2]).then_inc(o_scaled, 1)

            def end0_xT(b):
                m = Pair(b.n, b.off // 2 - 1)
                split_xT(b, b.after(1, 1), kq_mm if m.exists() else None, m.after(2, 2))

            def end0_v(b):
                act.wait_ge(v_mm, b.after(1, 1))
                if b.needs(1, -1):
                    act.wait_ge(v_stored[b.par], b.at(-2).landed())
                act.activation(v_hl[:, b.par, 0:D], E0[:, 0:D], ACT.Copy).then_inc(v_hi, 1)
                act.activation(f32(v_hl[:, b.par, D:2 * D]), E0[:, 0:D], ACT.Copy).then_inc(v_raw, 1)

            def end0_kq(m, which):
                act.wait_ge(kq_mm, m.after(2, which + 1))
                if m.needs(1, 0):
                    act.wait_ge(*((q_stored, m.after(16, 0)) if which else (k_placed, m.after(32, 0))))
                for g in range(DC):
                    product, b = E1[:, g * 2 * P:(g + 1) * 2 * P], bias_kq[:, which * DC + g:which * DC + g + 1]
                    act.activation(kq_hl[:, which, 0, g, :], product, ACT.Identity, bias=b).then_inc(kq_hi, 1)
                    act.activation(f32(kq_hl[:, which, 1, g, :]), product, ACT.Identity, bias=b).then_inc(kq_raw, 1)

            def split_x(c):
                act.wait_ge(x_stage_in[c], 16)
                act.activation(xhl[:, c * TPC:(c + 1) * TPC, 0:D], x_stage[:, c * TPC:(c + 1) * TPC, :],
                               ACT.Copy).then_inc(x_hi, 1)

            def split_weights():
                act.wait_ge(const_in, 32)
                act.wait_ge(bias_in, 48)
                act.activation(w_stage[:, :, D:2 * D], w_stage[:, :, D:2 * D], ACT.Copy,
                               scale=1.0 / 32.0).then_inc(w_hi, 1)
                act.activation(bias_kq[:, DC:2 * DC], bias_kq[:, DC:2 * DC], ACT.Copy,
                               scale=1.0 / 32.0).then_inc(w_hi, 1)
                act.wait_ge(w_hi, 2)
                act.activation(w_hl[:, 0, :, :], w_stage[:, :, :], ACT.Copy).then_inc(w_hi, 1)
                act.activation(b_r[:, :], b_stage[:, :], ACT.Copy).then_inc(w_hi, 1)

            def slot0(b, c):
                start = isinstance(b.n, int) and b.number == 0
                chunk_hi(b, c, t0_done, mm0, T0[c % 4], hi0)
                if start and c < CHUNKS - 1:
                    split_x(c + 1)
                if start and c == CHUNKS - 1:
                    split_weights()
                if b.at(-2).exists():
                    if c == 0:
                        end0_xT(b.at(-2))
                    if c == 6 and not b.par:
                        end0_v(b.at(-2))
                if b.at(-3).exists() and c == 2 and not b.par:
                    end0_v(b.at(-3))
                if b.at(-1).exists() and c == 3:
                    end0_scale(b.at(-1))
                if b.at(1).exists() and c in (0, 2, 3, 4):
                    row_sum(b.at(1), (0, 2, 3, 4).index(c))
                if b.at(-1).exists():
                    if c == 7:
                        normalise(0, b.at(-1))
                if b.par and Pair(b.n, b.off // 2 - 1).exists() and c in (4, 7):
                    end0_kq(Pair(b.n, b.off // 2 - 1), c // 7)

            for p in range(PIECES):
                row_sum(Blk(0, 0), p)
            split_x(0)
            for off in range(4):
                for c in range(CHUNKS):
                    slot0(Blk(0, off), c)
            with act.Fori(2, PAIRS - 1) as n:
                for off in range(2):
                    for c in range(CHUNKS):
                        slot0(Blk(n, off), c)
            for off in range(2):
                for c in range(CHUNKS):
                    slot0(Blk(PAIRS - 1, off), c)

            def probabilities(b, p):
                act.wait_ge(maxed, b.after(2, 2))
                a = a_buf[b.par][:, p * PW:(p + 1) * PW]
                act.activation(a, a, ACT.Exp, bias=mx[:, b.par, 1:2], scale=2.0,
                               accum_out=lp[:, b.par, p:p + 1]).then_inc(exped, 1)

            def end1(b, c):
                if c == 3:
                    normalise(1, b)
                if c == 6:
                    act.wait_ge(xw_mm, b.after(1, 1))
                    if isinstance(b.n, int) and b.number >= NB - 2:
                        act.activation(xw[:, b.number, :], E0[:, 0:D], ACT.Copy).then_inc(xw_copied, 1)
                        return
                    if b.needs(1, 0):
                        act.wait_ge(xw_stored, b.after(16, 0))
                    act.activation(xw_out[:, :], E0[:, 0:D], ACT.Copy).then_inc(xw_copied, 1)

            def slot1(b, c):
                t = b.at(-1) if c >= 1 else b.at(-2)
                if t.exists():
                    tc = (c - 1) % CHUNKS
                    chunk_hi(t, tc, t1_done, pv_done, T1[tc % 2], hi1)
                if b.at(-1).exists() and c % 2 == 0:
                    probabilities(b.at(-1), c // 2)
                if b.at(-2).exists():
                    if b.exists() or c != 3:
                        end1(b.at(-2), c if b.exists() or c < 3 else c - 1)

            def piece_hi(layer, b, p):
                act.wait_ge(a_in[b.par][p], b.landed(layer))
                if layer == 3 or b.needs(1, 0):
                    act.wait_ge(mm2, over(b, layer - 2, 4, p + 1) - 4)
                elif p == 0:
                    act.wait_ge(qk_done, 8 * NB)
                act.activation(piece_hl[:, p, 0, :], a_buf[b.par][:, p * PW:(p + 1) * PW],
                               ACT.Copy).then_inc(hi2, 1)

            for off in range(2):
                for c in range(CHUNKS):
                    if off == 0:
                        if c == 0:
                            end0_xT(Blk(0, NB - 2))
                            end0_v(Blk(0, NB - 3))
                            end0_scale(Blk(0, NB - 1))
                            end0_v(Blk(0, NB - 2))
                            normalise(0, Blk(0, NB - 1))
                        if c == 2:
                            end0_xT(Blk(0, NB - 1))
                        if c == 3:
                            end0_kq(Pair(0, PAIRS - 1), 0)
                            end0_v(Blk(0, NB - 1))
                        if c == 6:
                            end0_kq(Pair(0, PAIRS - 1), 1)
                    if off == 1 and c == 7:
                        act.wait_ge(w23_in, 32)
                        act.activation(w3_hl[:, 0, :, :], w3_stage[:, :, :], ACT.Copy).then_inc(w3_hi, 1)
                    slot1(Blk(0, off), c)
            with act.Fori(1, PAIRS) as n:
                for off in range(2):
                    for c in range(CHUNKS):
                        slot1(Blk(n, off), c)
            for c in range(CHUNKS):
                slot1(Blk(0, NB), c)
                if c % 2:
                    piece_hi(2, Blk(0, 0), c // 2)
            for c in range(1):
                slot1(Blk(0, NB + 1), c)

            def y_split(b):
                act.wait_ge(y_mm, b.after(1, 1))
                act.activation(yhl[:, b.rows(), 0:D], E0[:, 0:D], ACT.Copy,
                               scale=dinv[:, bass.ds(b.rows(), 1)]).then_inc(y_hi, 1)

            def body2(layer, b, has_next=True):
                prev_layer, prev = ahead(layer, b, -1)
                for p in range(PIECES):
                    if p == 2 and prev_layer == 1:
                        end1(prev, 6)
                    if p == 2 and (prev_layer, layer) == (2, 3):
                        y_split(prev)
                    if has_next:
                        piece_hi(layer, b.at(1), p)
                    if p == 0 and prev_layer > 1:
                        normalise(prev_layer, prev)
                    if p == 1 and prev_layer == 2:
                        split_xT(prev, over(prev, 2, 1, 1), y_mm if prev.needs(1, 0) else None, prev.after(1, 0))
                    if p == 3 and layer == prev_layer == 2:
                        y_split(prev)

            end1(Blk(0, NB - 1), 3)
            for layer in (2, 3):
                for off in range(2):
                    body2(layer, Blk(0, off))
                with act.Fori(1, PAIRS - 1) as n:
                    for off in range(2):
                        body2(layer, Blk(n, off))
                for off in range(2):
                    body2(layer, Blk(PAIRS - 1, off), has_next=(layer, off) != (3, 1))
            normalise(3, Blk(0, NB - 1))

        @block.vector
        def _(dve):
            def settled(b, i):
                if not isinstance(b.n, int):
                    dve.memset(settle[0:1, i:i + 1], 0.0)

            def count(b, p):
                dve.wait_ge(a_in[b.par][p], b.landed())
                if b.needs(1, -1):
                    dve.wait_ge(stats, b.at(-2).after(10, 1))
                if b.at(-1).exists():
                    dve.wait_ge(inc_done, b.at(-1).after(8, 2 * p + 2))
                dve.tensor_scalar(mask[:, p * PW:(p + 1) * PW], a_buf[b.par][:, p * PW:(p + 1) * PW], 0.0, 0.0, ALU.is_gt,
                                  ALU.add, accum_out=part[:, b.par, 0, p:p + 1]).then_inc(counted, 1)

            def scale_of_head(b):
                dve.wait_ge(stats, b.after(10, 4))
                if b.needs(1, -1):
                    dve.wait_ge(stats, b.at(-2).after(10, 10))
                dve.tensor_scalar(rr[:, b.par, 0:1], st[:, b.par, 2:3], HEAD_EPS, None,
                                  ALU.max).then_inc(head_scale, 1)
                dve.tensor_scalar(rr[:, b.par, 3:4], st[:, b.par, 3:4], 0.0, None,
                                  ALU.is_equal).then_inc(head_scale, 1)

            def reciprocal_degree(b):
                dve.wait_ge(stats, b.after(10, 10))
                dve.reciprocal(rr[:, b.par, 1:2], st[:, b.par, 9:10]).then_inc(rdeg, 1)

            def scaled_inc(b, c):
                if c == 0:
                    dve.wait_ge(head_scale, b.after(2, 2))
                dve.wait_ge(counted, b.after(4, c // 2 + 1))
                a = a_buf[b.par][:, c * CW:(c + 1) * CW]
                dve.scalar_tensor_tensor(a, a, rr[:, b.par, 0:1], mask[:, c * CW:(c + 1) * CW], ALU.mult,
                                         ALU.add).then_inc(inc_done, 1)

            def chunk_lo(b, c, hi_sem, t_bank, out_sem):
                dve.wait_ge(hi_sem, b.after(8, c + 1))
                dve.tensor_tensor(chunk_hl[:, c % 4, 1, :], t_bank[:, :], f32(chunk_hl[:, c % 4, 0, :]),
                                  ALU.subtract).then_inc(out_sem, 1)

            def moments(layer, b, k):
                partial_moments(layer, b, k)
                whole_moments(layer, b, k)

            def partial_moments(layer, b, k):
                dve.wait_ge(ln[layer], b.after(LN_STEPS[layer], k))
                dve.bn_stats(bn6[:, :], u[:, :]).then_inc(ln[layer], 1)

            def whole_moments(layer, b, k):
                s, steps = ln[layer], LN_STEPS[layer]
                dve.wait_ge(s, b.after(steps, k + 1))
                if layer > 0 or b.needs(1, 0):
                    dve.wait_ge(normed, over(b, layer, 4, 0))
                settled(b, CHUNKS)
                dve.bn_aggr(mv[:, :], bn6[:, :]).then_inc(s, 1)

            def start_end(layer, b):
                dve.wait_ge(xres_in[b.par], b.landed(layer))
                if layer > 0 or b.needs(1, 0):
                    dve.wait_ge(xn_done, over(b, layer, 1, 0))

            def add_scaled(layer, b, k, scale):
                s, steps, o = ln[layer], LN_STEPS[layer], O[b.par]
                dve.scalar_tensor_tensor(u[:, :], o[:, 0:D], scale, xres[:, b.par, :], ALU.mult,
                                         ALU.add).then_inc(s, 1)
                dve.wait_ge(s, b.after(steps, k + 1))
                dve.scalar_tensor_tensor(u[:, :], o[:, D:2 * D], scale, u[:, :], ALU.mult,
                                         ALU.add).then_inc(s, 1)

            def split_xT(b, t_value):
                dve.wait_ge(xT_hi, t_value)
                dve.tensor_tensor(xT[:, 1, :, b.par, :], E0[:, 0:D].rearrange("p (c i) -> p c i", c=DC),
                                  f32(xT[:, 0, :, b.par, :]), ALU.subtract).then_inc(xT_lo, 1)

            def end0_u(b):
                dve.wait_ge(o_plus_x, b.after(1, 1))
                dve.scalar_tensor_tensor(u[:, :], O[b.par][:, D:2 * D], rr[:, b.par, 1:2], u[:, :], ALU.mult,
                                         ALU.add).then_inc(ln[0], 1)

            def slot0(b, c):
                nxt, prev = b.at(1), b.at(-1)
                if c < 5:
                    scaled_inc(b, c + 3)
                if c == 4 and prev.exists():
                    end0_u(prev)
                if c == 5 and prev.exists():
                    whole_moments(0, prev, 1)
                if c == 6 and nxt.exists():
                    scale_of_head(nxt)
                chunk_lo(b, c, hi0, T0[c % 4], lo0)
                if c == 0 and b.at(-2).exists():
                    split_xT(b.at(-2), b.at(-2).after(1, 1))
                if c == 1:
                    reciprocal_degree(b)
                if nxt.exists() and c in (0, 1, 3, 4):
                    count(nxt, (0, 1, 3, 4).index(c))
                if c == 4 and prev.exists():
                    partial_moments(0, prev, 1)
                if nxt.exists() and c >= 6:
                    scaled_inc(nxt, c - 6)
                if c == 7 and nxt.exists():
                    scaled_inc(nxt, 2)

            for p in range(PIECES):
                count(Blk(0, 0), p)
            scale_of_head(Blk(0, 0))
            for c in range(3):
                scaled_inc(Blk(0, 0), c)
            for off in range(2):
                for c in range(CHUNKS):
                    slot0(Blk(0, off), c)
            with dve.Fori(1, PAIRS - 1) as n:
                for off in range(2):
                    for c in range(CHUNKS):
                        slot0(Blk(n, off), c)
            for off in range(2):
                for c in range(CHUNKS):
                    slot0(Blk(PAIRS - 1, off), c)

            def add_adj(b, c):
                dve.wait_ge(qk_done, b.after(8, c + 1))
                dve.wait_ge(a_in[b.par][c // 2], b.landed(1))
                a = a_buf[b.par][:, c * CW:(c + 1) * CW]
                settled(b, c)
                dve.tensor_tensor_reduce(a, S1[c % 2][:, :], a, 1.0, -3.0e38, ALU.add, ALU.max,
                                         mxp[:, b.par, c:c + 1]).then_inc(scored, 1)

            def row_max(b):
                dve.wait_ge(scored, b.after(8, 8))
                dve.tensor_reduce(mx[:, b.par, 0:1], mxp[:, b.par, :], AX.X, ALU.max).then_inc(maxed, 1)
                dve.wait_ge(maxed, b.after(2, 1))
                if b.needs(1, -1):
                    dve.wait_ge(exped, b.at(-2).after(4, 4))
                dve.tensor_scalar(mx[:, b.par, 1:2], mx[:, b.par, 0:1], -2.0, None, ALU.mult).then_inc(maxed, 1)

            def end1(b, c):
                if c == 2:
                    start_end(1, b)
                    dve.wait_ge(exped, b.after(4, 4))
                    dve.tensor_reduce(ls[:, 0:1], lp[:, b.par, :], AX.X, ALU.add).then_inc(ln[1], 1)
                    dve.wait_ge(ln[1], b.after(6, 1))
                    dve.reciprocal(ls[:, 1:2], ls[:, 0:1]).then_inc(ln[1], 1)
                    dve.wait_ge(ln[1], b.after(6, 2))
                    dve.wait_ge(pv_done, b.after(8, 8))
                    add_scaled(1, b, 2, ls[:, 1:2])
                    moments(1, b, 4)
                if c == 4:
                    dve.wait_ge(xn_done, over(b, 1, 1, 1))
                    if b.needs(1, 0):
                        dve.wait_ge(xT_done, over(b, 1, 1, 0))
                    dve.tensor_scalar(ba[:, :], xn[:, b.par, :], 0.0, None, ALU.is_gt).then_inc(bin_done, 1)
                if c == 5:
                    dve.wait_ge(xT_done, over(b, 1, 1, 1))
                    if b.needs(1, 0):
                        dve.wait_ge(xw_mm, b.after(1, 0))
                    dve.tensor_copy(baT[:, :, :].rearrange("p c n -> p (c n)"), E0[:, 0:D]).then_inc(binT_done, 1)

            def slot1(b, c):
                if b.exists():
                    add_adj(b, c)
                    if c == CHUNKS - 1:
                        row_max(b)
                t = b.at(-1) if c >= 1 else b.at(-2)
                if t.exists():
                    tc = (c - 1) % CHUNKS
                    chunk_lo(t, tc, hi1, T1[tc % 2], lo1)
                if b.at(-2).exists():
                    if b.exists() or c != 3:
                        end1(b.at(-2), c if b.exists() or c < 3 else c - 1)

            for off in range(2):
                for c in range(CHUNKS):
                    if off == 0:
                        if c == 0:
                            split_xT(Blk(0, NB - 2), NB - 1)
                            end0_u(Blk(0, NB - 1))
                            moments(0, Blk(0, NB - 1), 1)
                    if off == 1 and c == 7:
                        dve.wait_ge(w23_in, 32)
                        dve.tensor_scalar(w2_sign[:, :, :], w2_stage[:, :, :], 0.0, None, ALU.is_lt).then_inc(w23_ready, 1)
                        dve.wait_ge(w23_ready, 1)
                        dve.scalar_tensor_tensor(w2_sign[:, :, :], w2_stage[:, :, :], 0.0,
                                                 f32(w2_sign[:, :, :]), ALU.is_gt,
                                                 ALU.subtract).then_inc(w23_ready, 1)
                        dve.wait_ge(w3_hi, 1)
                        dve.tensor_tensor(w3_hl[:, 1, :, :], w3_stage[:, :, :], f32(w3_hl[:, 0, :, :]),
                                          ALU.subtract).then_inc(w23_ready, 1)
                    slot1(Blk(0, off), c)
                    if off == 0:
                        if c == 2:
                            split_xT(Blk(0, NB - 1), NB)
            with dve.Fori(1, PAIRS) as n:
                for off in range(2):
                    for c in range(CHUNKS):
                        slot1(Blk(n, off), c)
            def piece_lo(layer, b, p):
                dve.wait_ge(hi2, over(b, layer - 2, 4, p + 1))
                dve.tensor_tensor(piece_hl[:, p, 1, :], a_buf[b.par][:, p * PW:(p + 1) * PW],
                                  f32(piece_hl[:, p, 0, :]), ALU.subtract).then_inc(lo2, 1)

            for c in range(CHUNKS):
                slot1(Blk(0, NB), c)
                if c % 2:
                    piece_lo(2, Blk(0, 0), c // 2)
            for c in range(1):
                slot1(Blk(0, NB + 1), c)

            def end2(b, stage):
                if stage == 0:
                    start_end(2, b)
                    dve.wait_ge(mm2, b.after(4, 4))
                    dve.scalar_tensor_tensor(u[:, :], O[b.par][:, 0:D], 0.0, xres[:, b.par, :], ALU.max,
                                             ALU.add).then_inc(ln[2], 1)
                    moments(2, b, 1)
                if stage == 1:
                    split_xT(b, over(b, 1, 1, 1))
                if stage == 2:
                    dve.wait_ge(y_hi, b.after(1, 1))
                    dve.scalar_tensor_tensor(yhl[:, b.rows(), D:2 * D], E0[:, 0:D],
                                             dinv[:, bass.ds(b.rows(), 1)], f32(yhl[:, b.rows(), 0:D]),
                                             ALU.mult, ALU.subtract).then_inc(y_lo, 1)

            def end3(b):
                s, o = ln[3], O[b.par]
                start_end(3, b)
                dve.wait_ge(mm2, over(b, 1, 4, 4))
                dve.tensor_tensor(u[:, :], o[:, 0:D], f32(yhl[:, b.rows(), 0:D]), ALU.add).then_inc(s, 1)
                dve.wait_ge(s, b.after(7, 1))
                dve.tensor_tensor(u[:, :], o[:, D:2 * D], u[:, :], ALU.add).then_inc(s, 1)
                dve.wait_ge(s, b.after(7, 2))
                dve.tensor_tensor(u[:, :], u[:, :], f32(yhl[:, b.rows(), D:2 * D]), ALU.add).then_inc(s, 1)
                dve.wait_ge(s, b.after(7, 3))
                dve.tensor_scalar(u[:, :], u[:, :], 0.0, dinv[:, bass.ds(b.rows(), 1)], ALU.max,
                                  ALU.mult).then_inc(s, 1)
                dve.wait_ge(s, b.after(7, 4))
                dve.tensor_tensor(u[:, :], u[:, :], xres[:, b.par, :], ALU.add).then_inc(s, 1)
                moments(3, b, 5)

            def body2(layer, b, has_next=True):
                prev_layer, prev = ahead(layer, b, -1)
                for p in range(PIECES):
                    if p == 1 and prev_layer == 1:
                        end1(prev, 5)
                    if p == 2 and (prev_layer, layer) == (2, 3):
                        end2(prev, 2)
                    if p == 3:
                        if layer == 2:
                            end2(b, 0)
                        else:
                            end3(b)
                    if has_next:
                        piece_lo(layer, b.at(1), p)
                    if p == 1 and prev_layer == 2:
                        end2(prev, 1)
                    if p == 3 and layer == prev_layer == 2:
                        end2(prev, 2)

            end1(Blk(0, NB - 1), 2)
            end1(Blk(0, NB - 1), 4)
            for layer in (2, 3):
                for off in range(2):
                    body2(layer, Blk(0, off))
                with dve.Fori(1, PAIRS - 1) as n:
                    for off in range(2):
                        body2(layer, Blk(n, off))
                for off in range(2):
                    body2(layer, Blk(PAIRS - 1, off), has_next=(layer, off) != (3, 1))

        @block.gpsimd
        def _(pool):
            pool.memset(f32(ones[:, :]), 1.0).then_inc(memsets, 1)
            for i, value in enumerate(CONSTANTS[:-1]):
                pool.memset(const[:, i:i + 1], value)
            pool.memset(const[:, len(CONSTANTS) - 1:], CONSTANTS[-1]).then_inc(memsets, 1)
            pool.memset(b_stage[:, :], 0.0).then_inc(memsets, 1)
            pool.wait_ge(memsets, 3)

            def row_sums(b):
                s, q = st[:, b.par, :], part[:, b.par, :, :]

                pool.wait_ge(counted, b.after(4, 4))
                pool.wait_ge(summed, b.after(4, 4))
                if b.needs(1, -1):
                    pool.wait_ge(rdeg, b.at(-2).after(1, 1))
                pool.tensor_tensor(st[:, b.par, 12:16].rearrange("p (a c) -> p a c", a=2), q[:, :, 0:2],
                                   q[:, :, 2:4], ALU.add).then_inc(stats, 1)
                pool.wait_ge(stats, b.after(10, 1))
                pool.tensor_tensor(s[:, 0:2], s[:, 12:16:2], s[:, 13:16:2], ALU.add).then_inc(stats, 1)
                pool.wait_ge(stats, b.after(10, 2))
                pool.tensor_tensor(s[:, 2:3], s[:, 0:1], const[:, C_HALF:C_HALF + 1],
                                   ALU.pow).then_inc(stats, 1)
                pool.tensor_tensor(s[:, 3:4], s[:, 1:2], const[:, C_ONE:C_ONE + 1],
                                   ALU.add).then_inc(stats, 1)

            def degrees(b):
                s = st[:, b.par, :]
                pool.wait_ge(head_scale, b.after(2, 2))
                pool.tensor_tensor(s[:, 5:6], s[:, 3:4], rr[:, b.par, 3:4], ALU.add).then_inc(stats, 1)
                pool.wait_ge(stats, b.after(10, 5))
                pool.tensor_tensor(s[:, 6:7], s[:, 5:6], const[:, C_MHALF:C_MHALF + 1],
                                   ALU.pow).then_inc(stats, 1)
                pool.tensor_tensor(s[:, 7:8], const[:, C_ONE:C_ONE + 1], rr[:, b.par, 3:4],
                                   ALU.subtract).then_inc(stats, 1)
                pool.wait_ge(stats, b.after(10, 7))
                pool.tensor_tensor(dinv[:, bass.ds(b.rows(), 1)], s[:, 6:7], s[:, 7:8],
                                   ALU.mult).then_inc(stats, 1)
                pool.tensor_tensor(s[:, 8:9], rr[:, b.par, 0:1], s[:, 1:2], ALU.mult).then_inc(stats, 1)
                pool.wait_ge(stats, b.after(10, 9))
                pool.tensor_tensor(s[:, 9:10], s[:, 8:9], s[:, 0:1], ALU.add).then_inc(stats, 1)

            def add_residual(b):
                pool.wait_ge(o_scaled, b.after(1, 1))
                pool.wait_ge(xres_in[b.par], b.landed())
                if b.needs(1, 0):
                    pool.wait_ge(xn_done, b.after(1, 0))
                pool.tensor_tensor(u[:, :], xn[:, b.par, :], xres[:, b.par, :], ALU.add).then_inc(o_plus_x, 1)

            def norm_statistics(layer, b):
                steps = LN_STEPS[layer]
                pool.wait_ge(ln[layer], b.after(steps, steps))
                if layer > 0 or b.needs(1, 0):
                    pool.wait_ge(xn_done, over(b, layer, 1, 0))
                pool.tensor_tensor(norm[:, 0:1], mv[:, 1:2], const[:, C_LN_EPS:C_LN_EPS + 1], ALU.add).then_inc(normed, 1)
                pool.tensor_tensor(norm[:, 3:4], const[:, C_ZERO:C_ZERO + 1], mv[:, 0:1], ALU.subtract).then_inc(normed, 1)
                pool.wait_ge(normed, over(b, layer, 4, 1))
                pool.tensor_tensor(norm[:, 1:2], norm[:, 0:1], const[:, C_MHALF:C_MHALF + 1], ALU.pow).then_inc(normed, 1)
                pool.wait_ge(normed, over(b, layer, 4, 3))
                pool.tensor_tensor(norm[:, 2:3], norm[:, 3:4], norm[:, 1:2], ALU.mult).then_inc(normed, 1)

            def v_low(b):
                pool.wait_ge(v_raw, b.after(1, 1))
                pool.tensor_tensor(v_hl[:, b.par, D:2 * D], f32(v_hl[:, b.par, D:2 * D]), f32(v_hl[:, b.par, 0:D]),
                                   ALU.subtract).then_inc(v_lo, 1)

            def kq_low(m, which):
                pool.wait_ge(kq_hi, m.after(4, 2 * which + 2))
                pool.wait_ge(kq_raw, m.after(4, 2 * which + 2))
                hi, lo = (kq_hl[:, which, h, :, :].rearrange("p c n -> p (c n)") for h in range(2))
                pool.tensor_tensor(lo, f32(lo), f32(hi), ALU.subtract).then_inc(kq_lo, 1)

            def split_x(c):
                pool.wait_ge(x_hi, c + 1)
                tiles = slice(c * TPC, (c + 1) * TPC)
                pool.tensor_tensor(xhl[:, tiles, D:2 * D], x_stage[:, tiles, :], f32(xhl[:, tiles, 0:D]),
                                   ALU.subtract).then_inc(x_lo, 1)

            row_sums(Blk(0, 0))
            degrees(Blk(0, 0))
            for c in range(CHUNKS - 2):
                split_x(c)
            row_sums(Blk(0, 1))
            degrees(Blk(0, 1))
            for c in range(CHUNKS - 2, CHUNKS):
                split_x(c)
            pool.wait_ge(w_hi, 4)
            pool.tensor_tensor(w_hl[:, 1, :, :], w_stage[:, :, :], f32(w_hl[:, 0, :, :]),
                               ALU.subtract).then_inc(w_lo, 1)
            pool.wait_ge(w_lo, 1)
            pool.tensor_tensor(b_r[32:33, :], b_stage[32:33, :], f32(b_r[32:33, :]),
                               ALU.subtract).then_inc(bias_ready, 1)
            pool.wait_ge(bias_ready, 1)
            def body0(b):
                pair = Pair(b.n, b.off // 2 - 2)
                if b.par and b.at(-4).exists():
                    v_low(b.at(-4))
                if b.at(-2).exists():
                    add_residual(b.at(-2))
                if b.exists():
                    row_sums(b)
                if b.at(-2).exists():
                    norm_statistics(0, b.at(-2))
                if b.exists():
                    degrees(b)
                if not b.par and pair.exists():
                    kq_low(pair, 0)
                    kq_low(pair, 1)
                if b.par and b.at(-3).exists():
                    v_low(b.at(-3))

            for off in range(2, 6):
                body0(Blk(0, off))
            with pool.Fori(3, PAIRS) as n:
                for off in range(2):
                    body0(Blk(n, off))
            body0(Blk(0, NB))
            v_low(Blk(0, NB - 3))
            add_residual(Blk(0, NB - 1))
            norm_statistics(0, Blk(0, NB - 1))
            v_low(Blk(0, NB - 2))
            kq_low(Pair(0, PAIRS - 1), 0)
            v_low(Blk(0, NB - 1))
            kq_low(Pair(0, PAIRS - 1), 1)
            for layer in range(1, 4):
                with pool.Fori(0, PAIRS) as n:
                    for off in range(2):
                        norm_statistics(layer, Blk(n, off))


def kernel(x, adj, L1_gnn_Wq, L1_gnn_bq, L1_gnn_Wk, L1_gnn_bk, L1_gnn_Wv, L1_gnn_bv, L2_gnn_weight,
           L3_gnn_weight):
    import numpy as np
    import concourse.bacc as bacc
    from concourse.bass_utils import run_bass_kernel_spmd

    x, adj = np.ascontiguousarray(x), np.ascontiguousarray(adj)
    arrays = {
        "x_in": x,
        "adj": adj,
        "adjT": np.ascontiguousarray(adj.reshape(NB, P, NB, P).transpose(0, 3, 2, 1)).reshape(NB, P, N),
        "wkqv": np.ascontiguousarray(np.concatenate(
            [np.asarray(w).T for w in (L1_gnn_Wk, L1_gnn_Wq, L1_gnn_Wv)], axis=1)),
        "bias_kq_in": np.ascontiguousarray(
            np.concatenate([np.asarray(b) for b in (L1_gnn_bk, L1_gnn_bq)]).reshape(2 * DC, P).T),
        "bias_v": np.asarray(L1_gnn_bv).reshape(1, D),
        "w2t": np.ascontiguousarray(np.asarray(L2_gnn_weight).T),
        "w3": np.ascontiguousarray(L3_gnn_weight),
        "ident_in": np.eye(P, dtype=np.float32),
    }
    nc = bacc.Bacc("TRN2", target_bir_lowering=False, num_devices=1, dynamic_dma_scratch_size=1024)
    args = {n: nc.dram_tensor(n, a.shape, mybir.dt.from_np(a.dtype), kind="ExternalInput").ap()
            for n, a in arrays.items()}
    args["out"] = nc.dram_tensor("out", (N, D), F32, kind="ExternalOutput").ap()
    build(nc, **args)
    r = run_bass_kernel_spmd(nc, [arrays], core_ids=[0])
    return r.results[0]["out"]
```
